# Optimizing a Trainium2 kernel written in Bass

```python
import numpy as np
import jax
import jax.numpy as jnp

def _softmax(x, axis=-1):
    return jax.nn.softmax(x, axis=axis)

def _gelu(x):
    return jax.nn.gelu(x, approximate=True)

def _silu(x):
    return jax.nn.silu(x)

def _sigmoid(x):
    return jax.nn.sigmoid(x)

def _layernorm(x, axis=-1, eps=1e-05):
    m = jnp.mean(x, axis=axis, keepdims=True)
    v = jnp.var(x, axis=axis, keepdims=True)
    return (x - m) / jnp.sqrt(v + eps)

def _scatter_add(tgt, idx, src, axis=0):
    return tgt.at[idx].add(src)

def _segment_sum(src, seg, n):
    return jax.ops.segment_sum(src, seg, n)
kernel_name = 'mk_hybrid_d1_jaxref_r8_61ff16'

def setup_inputs(seed: int=0):
    np.random.seed(seed)
    _w = jnp.asarray

    def _L0_attn_a_setup():
        import jax, jax.numpy as jnp
        import numpy as np
        import math
        from jax import lax
        B, T, HID, H, J = (4, 256, 128, 8, 2)
        EPS = 1e-06
        LN_EPS = 1e-05

        def _alibi_slopes(n):

            def pow2(m):
                start = 2 ** (-2 ** (-(math.log2(m) - 3)))
                return [start * start ** i for i in range(m)]
            if math.log2(n).is_integer():
                return np.array(pow2(n), dtype=np.float32)
            c = 2 ** int(math.floor(math.log2(n)))
            s = pow2(c) + _alibi_slopes(2 * c).tolist()[:n - c]
            return np.array(s, dtype=np.float32)

        def _deltanet(x, Wq, Wk, Wv, Wbeta, bbeta, Wmix, bmix, Wgate, bgate, Wout, bout, ln_g, ln_b):
            b, t, hid = x.shape
            h = Wgate.shape[0]
            j = Wbeta.shape[0] // h
            d = hid // h
            r = jnp.asarray(np.exp(-_alibi_slopes(h)))[None, :, None]
            q = (jax.nn.elu(x @ Wq.T) + 1.0).reshape(b, t, h, d)
            k = (jax.nn.elu(x @ Wk.T) + 1.0).reshape(b, t, h, d)
            v = (x @ Wv.T).reshape(b, t, h, d)
            beta = (x @ Wbeta.T + bbeta).reshape(b, t, h, j)
            mix = (x @ Wmix.T + bmix).reshape(b, t, h, j)
            gate = jax.nn.sigmoid(x @ Wgate.T + bgate)

            def step(carry, inp):
                S, z = carry
                q_t, k_t, v_t, beta_t, mix_t, g_t = inp
                beta_eff = jnp.minimum(jax.nn.sigmoid(beta_t) * r, 0.9999)
                outer = jnp.einsum('bhd,bhe->bhde', k_t, v_t).astype(jnp.float32)[:, :, None]
                S = S * beta_eff[..., None, None] + g_t[:, :, None, None, None] * outer
                z = z * beta_eff[..., None] + g_t[:, :, None, None] * k_t[:, :, None, :]
                num = jnp.einsum('bhd,bhjde->bhje', q_t, S)
                denom = jnp.einsum('bhd,bhjd->bhj', q_t, z) + EPS
                w = jax.nn.softmax(mix_t, axis=-1)[..., None]
                y_t = jnp.sum(num / denom[..., None] * w, axis=2)
                return ((S, z), y_t)
            S0 = jnp.zeros((b, h, j, d, d), jnp.float32)
            z0 = jnp.zeros((b, h, j, d), jnp.float32)
            tm = lambda a: jnp.swapaxes(a, 0, 1)
            _, yT = lax.scan(step, (S0, z0), (tm(q), tm(k), tm(v), tm(beta), tm(mix), tm(gate)))
            y = jnp.swapaxes(yT, 0, 1).reshape(b, t, hid).astype(x.dtype)
            out = y @ Wout.T + bout
            hres = x + out
            mu = jnp.mean(hres, axis=-1, keepdims=True)
            var = jnp.mean(jnp.square(hres - mu), axis=-1, keepdims=True)
            return (hres - mu) / jnp.sqrt(var + LN_EPS) * ln_g + ln_b
        key = jax.random.key(seed)
        ks = jax.random.split(key, 9)
        sc = 0.02
        return {'x': jax.random.normal(ks[0], (B, T, HID), jnp.float32), 'Wq': jax.random.normal(ks[1], (HID, HID), jnp.float32) * sc, 'Wk': jax.random.normal(ks[2], (HID, HID), jnp.float32) * sc, 'Wv': jax.random.normal(ks[3], (HID, HID), jnp.float32) * sc, 'Wbeta': jax.random.normal(ks[4], (H * J, HID), jnp.float32) * sc, 'bbeta': jnp.full((H * J,), 2.1972, jnp.float32), 'Wmix': jax.random.normal(ks[5], (H * J, HID), jnp.float32) * sc, 'bmix': jnp.zeros((H * J,), jnp.float32), 'Wgate': jax.random.normal(ks[6], (H, HID), jnp.float32) * sc, 'bgate': jnp.zeros((H,), jnp.float32), 'Wout': jax.random.normal(ks[7], (HID, HID), jnp.float32) * sc, 'bout': jnp.zeros((HID,), jnp.float32), 'ln_g': jnp.ones((HID,), jnp.float32), 'ln_b': jnp.zeros((HID,), jnp.float32)}
    _L0_attn_a_in = _L0_attn_a_setup()

    def _L0_attn_b_setup():
        import jax, jax.numpy as jnp
        import numpy as np
        D_MODEL = 128
        N_HEADS = 16
        D_HEAD = D_MODEL // N_HEADS
        ROPE_BASE = 10000.0

        def _rope_cos_sin(seq_len, dtype):
            inv_freq = 1.0 / ROPE_BASE ** (jnp.arange(0, D_HEAD, 2, dtype=jnp.float32) / D_HEAD)
            t = jnp.arange(seq_len, dtype=jnp.float32)
            freqs = jnp.einsum('t,d->td', t, inv_freq)
            freqs = jnp.concatenate([freqs, freqs], axis=-1)
            return (jnp.cos(freqs).astype(dtype), jnp.sin(freqs).astype(dtype))

        def _rotate_half(x):
            x1, x2 = jnp.split(x, 2, axis=-1)
            return jnp.concatenate([-x2, x1], axis=-1)
        key = jax.random.key(seed)
        k1, k2, k3, k4, k5 = jax.random.split(key, 5)
        std = 0.02 / np.sqrt(2 * 12)
        x = jax.random.normal(k1, (2, 256, D_MODEL), dtype=jnp.float32)
        qkv_w = jax.random.normal(k2, (3 * D_MODEL, D_MODEL), dtype=jnp.float32) * std
        qkv_b = jnp.zeros((3 * D_MODEL,), dtype=jnp.float32)
        proj_w = jax.random.normal(k3, (D_MODEL, D_MODEL), dtype=jnp.float32) * std
        proj_b = jnp.zeros((D_MODEL,), dtype=jnp.float32)
        return {'x': x, 'qkv_w': qkv_w, 'qkv_b': qkv_b, 'proj_w': proj_w, 'proj_b': proj_b}
    _L0_attn_b_in = _L0_attn_b_setup()

    def _L0_ffn_setup():
        import jax, jax.numpy as jnp
        import numpy as np
        key = jax.random.key(seed)
        kx, kw = jax.random.split(key)
        x = jax.random.normal(kx, (32, 512, 128), dtype=jnp.float32)
        weight = jax.random.normal(kw, (128, 128), dtype=jnp.float32) * 0.01
        return {'x': x, 'weight': weight}
    _L0_ffn_in = _L0_ffn_setup()
    _d = {'L0_attn_a_x': _L0_attn_a_in['x'], 'L0_attn_a_Wq': _L0_attn_a_in['Wq'], 'L0_attn_a_Wk': _L0_attn_a_in['Wk'], 'L0_attn_a_Wv': _L0_attn_a_in['Wv'], 'L0_attn_a_Wbeta': _L0_attn_a_in['Wbeta'], 'L0_attn_a_bbeta': _L0_attn_a_in['bbeta'], 'L0_attn_a_Wmix': _L0_attn_a_in['Wmix'], 'L0_attn_a_bmix': _L0_attn_a_in['bmix'], 'L0_attn_a_Wgate': _L0_attn_a_in['Wgate'], 'L0_attn_a_bgate': _L0_attn_a_in['bgate'], 'L0_attn_a_Wout': _L0_attn_a_in['Wout'], 'L0_attn_a_bout': _L0_attn_a_in['bout'], 'L0_attn_a_ln_g': _L0_attn_a_in['ln_g'], 'L0_attn_a_ln_b': _L0_attn_a_in['ln_b'], 'L0_attn_b_qkv_w': _L0_attn_b_in['qkv_w'], 'L0_attn_b_qkv_b': _L0_attn_b_in['qkv_b'], 'L0_attn_b_proj_w': _L0_attn_b_in['proj_w'], 'L0_attn_b_proj_b': _L0_attn_b_in['proj_b'], 'L0_ffn_weight': _L0_ffn_in['weight']}
    _x0 = _d['L0_attn_a_x']
    _d['L0_attn_a_x'] = jax.random.normal(jax.random.fold_in(jax.random.key(seed), 1), (8, 512, 128), dtype=_x0.dtype)
    del _x0
    return _d

def reference(L0_attn_a_x, L0_attn_a_Wq, L0_attn_a_Wk, L0_attn_a_Wv, L0_attn_a_Wbeta, L0_attn_a_bbeta, L0_attn_a_Wmix, L0_attn_a_bmix, L0_attn_a_Wgate, L0_attn_a_bgate, L0_attn_a_Wout, L0_attn_a_bout, L0_attn_a_ln_g, L0_attn_a_ln_b, L0_attn_b_qkv_w, L0_attn_b_qkv_b, L0_attn_b_proj_w, L0_attn_b_proj_b, L0_ffn_weight):

    def _L0_attn_a_ref(x, Wq, Wk, Wv, Wbeta, bbeta, Wmix, bmix, Wgate, bgate, Wout, bout, ln_g, ln_b):
        import jax, jax.numpy as jnp
        import numpy as np
        import math
        from jax import lax
        B, T, HID, H, J = (4, 256, 128, 8, 2)
        EPS = 1e-06
        LN_EPS = 1e-05

        def _alibi_slopes(n):

            def pow2(m):
                start = 2 ** (-2 ** (-(math.log2(m) - 3)))
                return [start * start ** i for i in range(m)]
            if math.log2(n).is_integer():
                return np.array(pow2(n), dtype=np.float32)
            c = 2 ** int(math.floor(math.log2(n)))
            s = pow2(c) + _alibi_slopes(2 * c).tolist()[:n - c]
            return np.array(s, dtype=np.float32)

        def _deltanet(x, Wq, Wk, Wv, Wbeta, bbeta, Wmix, bmix, Wgate, bgate, Wout, bout, ln_g, ln_b):
            b, t, hid = x.shape
            h = Wgate.shape[0]
            j = Wbeta.shape[0] // h
            d = hid // h
            r = jnp.asarray(np.exp(-_alibi_slopes(h)))[None, :, None]
            q = (jax.nn.elu(x @ Wq.T) + 1.0).reshape(b, t, h, d)
            k = (jax.nn.elu(x @ Wk.T) + 1.0).reshape(b, t, h, d)
            v = (x @ Wv.T).reshape(b, t, h, d)
            beta = (x @ Wbeta.T + bbeta).reshape(b, t, h, j)
            mix = (x @ Wmix.T + bmix).reshape(b, t, h, j)
            gate = jax.nn.sigmoid(x @ Wgate.T + bgate)

            def step(carry, inp):
                S, z = carry
                q_t, k_t, v_t, beta_t, mix_t, g_t = inp
                beta_eff = jnp.minimum(jax.nn.sigmoid(beta_t) * r, 0.9999)
                outer = jnp.einsum('bhd,bhe->bhde', k_t, v_t).astype(jnp.float32)[:, :, None]
                S = S * beta_eff[..., None, None] + g_t[:, :, None, None, None] * outer
                z = z * beta_eff[..., None] + g_t[:, :, None, None] * k_t[:, :, None, :]
                num = jnp.einsum('bhd,bhjde->bhje', q_t, S)
                denom = jnp.einsum('bhd,bhjd->bhj', q_t, z) + EPS
                w = jax.nn.softmax(mix_t, axis=-1)[..., None]
                y_t = jnp.sum(num / denom[..., None] * w, axis=2)
                return ((S, z), y_t)
            S0 = jnp.zeros((b, h, j, d, d), jnp.float32)
            z0 = jnp.zeros((b, h, j, d), jnp.float32)
            tm = lambda a: jnp.swapaxes(a, 0, 1)
            _, yT = lax.scan(step, (S0, z0), (tm(q), tm(k), tm(v), tm(beta), tm(mix), tm(gate)))
            y = jnp.swapaxes(yT, 0, 1).reshape(b, t, hid).astype(x.dtype)
            out = y @ Wout.T + bout
            hres = x + out
            mu = jnp.mean(hres, axis=-1, keepdims=True)
            var = jnp.mean(jnp.square(hres - mu), axis=-1, keepdims=True)
            return (hres - mu) / jnp.sqrt(var + LN_EPS) * ln_g + ln_b
        return _deltanet(x, Wq, Wk, Wv, Wbeta, bbeta, Wmix, bmix, Wgate, bgate, Wout, bout, ln_g, ln_b)

    def _L0_attn_b_ref(x, qkv_w, qkv_b, proj_w, proj_b):
        import jax, jax.numpy as jnp
        import numpy as np
        D_MODEL = 128
        N_HEADS = 16
        D_HEAD = D_MODEL // N_HEADS
        ROPE_BASE = 10000.0

        def _rope_cos_sin(seq_len, dtype):
            inv_freq = 1.0 / ROPE_BASE ** (jnp.arange(0, D_HEAD, 2, dtype=jnp.float32) / D_HEAD)
            t = jnp.arange(seq_len, dtype=jnp.float32)
            freqs = jnp.einsum('t,d->td', t, inv_freq)
            freqs = jnp.concatenate([freqs, freqs], axis=-1)
            return (jnp.cos(freqs).astype(dtype), jnp.sin(freqs).astype(dtype))

        def _rotate_half(x):
            x1, x2 = jnp.split(x, 2, axis=-1)
            return jnp.concatenate([-x2, x1], axis=-1)
        B, S, D = x.shape
        H, Dh = (N_HEADS, D_HEAD)
        scale = 1.0 / np.sqrt(Dh)
        qkv = x @ qkv_w.T + qkv_b
        qkv = qkv.reshape(B, S, 3, H, Dh)
        q = jnp.transpose(qkv[:, :, 0], (0, 2, 1, 3))
        k = jnp.transpose(qkv[:, :, 1], (0, 2, 1, 3))
        v = jnp.transpose(qkv[:, :, 2], (0, 2, 1, 3))
        cos, sin = _rope_cos_sin(S, x.dtype)
        q = q * cos + _rotate_half(q) * sin
        k = k * cos + _rotate_half(k) * sin
        scores = jnp.einsum('bhsd,bhtd->bhst', q, k) * scale
        causal = jnp.triu(jnp.ones((S, S), dtype=bool), k=1)
        neg = jnp.finfo(scores.dtype).min
        scores = jnp.where(causal[None, None], neg, scores)
        probs = jax.nn.softmax(scores, axis=-1)
        ctx = jnp.einsum('bhst,bhtd->bhsd', probs, v)
        out = jnp.transpose(ctx, (0, 2, 1, 3)).reshape(B, S, D)
        out = out @ proj_w.T + proj_b
        return out

    def _L0_ffn_ref(x, weight):
        import jax, jax.numpy as jnp
        import numpy as np
        b_weight = jnp.sign(weight)
        return jnp.einsum('bsi,oi->bso', x, b_weight)
    x = L0_attn_a_x
    x = x + _L0_attn_a_ref(_layernorm(x, axis=-1), L0_attn_a_Wq, L0_attn_a_Wk, L0_attn_a_Wv, L0_attn_a_Wbeta, L0_attn_a_bbeta, L0_attn_a_Wmix, L0_attn_a_bmix, L0_attn_a_Wgate, L0_attn_a_bgate, L0_attn_a_Wout, L0_attn_a_bout, L0_attn_a_ln_g, L0_attn_a_ln_b)
    x = x + _L0_ffn_ref(_layernorm(x, axis=-1), L0_ffn_weight)
    x = x + _L0_attn_b_ref(_layernorm(x, axis=-1), L0_attn_b_qkv_w, L0_attn_b_qkv_b, L0_attn_b_proj_w, L0_attn_b_proj_b)
    x = x + _L0_ffn_ref(_layernorm(x, axis=-1), L0_ffn_weight)
    return x

_drawn_inputs = setup_inputs


def setup_inputs(seed=0):
    import zlib

    import numpy as np

    out = dict(_drawn_inputs(seed))
    spreads = {'L0_attn_a_bbeta': (2.197200059890747, 0.6),
     'L0_attn_a_bmix': (0.0, 2.0),
     'L0_attn_a_bgate': (0.0, 0.8),
     'L0_attn_a_bout': (0.0, 0.1),
     'L0_attn_a_ln_g': (1.0, 0.2),
     'L0_attn_a_ln_b': (0.0, 0.1),
     'L0_attn_b_qkv_b': (0.0, 2.0),
     'L0_attn_b_proj_b': (0.0, 0.786)}
    factors = {'L0_attn_a_Wq': 8.0,
     'L0_attn_a_Wk': 8.0,
     'L0_attn_a_Wv': 6.267,
     'L0_attn_a_Wbeta': 8.0,
     'L0_attn_a_Wmix': 8.0,
     'L0_attn_a_Wgate': 8.0,
     'L0_attn_a_Wout': 6.334,
     'L0_attn_b_qkv_w': 64.0,
     'L0_attn_b_proj_w': 8.0}
    for name, (base, spread) in spreads.items():
        noise = np.random.default_rng([zlib.crc32(name.encode()), seed]).standard_normal(out[name].shape)
        drawn = base * np.exp(spread * noise) if base else spread * noise
        out[name] = jnp.asarray(drawn.astype(out[name].dtype))
    for name, factor in factors.items():
        out[name] = (out[name] * factor).astype(out[name].dtype)
    return out
```

```python
import math
from contextlib import ExitStack

import numpy as np

import concourse.bass as bass
from concourse import mybir

F32 = mybir.dt.float32
BF16 = mybir.dt.bfloat16
ALU = mybir.AluOpType
ACT = mybir.ActivationFunctionType
AX = mybir.AxisListType

B, T, D = 8, 512, 128
P = 128
C = T // P
H, J, DH = 8, 2, 16
HJ = H * J
QUAD = 32
HA, DA = 16, 8
LN_EPS = 1e-5
DEN_EPS = 1e-6
BETA_CAP = math.log(0.9999)
SCALE = 1.0 / math.sqrt(DA)
NEG = -3.0e38

W_Q, W_K, W_V = 0, 128, 256
W_GATES = 384
N_GATES = 2 * HJ + H
W_OUT = W_GATES + N_GATES
W_FFN = W_OUT + D
W_QKV = W_FFN + D
W_PROJ = W_QKV + 3 * D
N_W = W_PROJ + D
N_TOK = 2 * D + N_GATES

V_GATES, V_BOUT, V_LNG, V_LNB, V_QKV = 0, 40, 168, 296, 424
V_PROJ = V_QKV + 3 * D
N_V = V_PROJ + D

C_ID, C_TRI, C_AFTER = 0, 128, 256
C_HEAD = 384
C_SLOPE = C_HEAD + H
C_COS = C_SLOPE + HJ
C_SIN = C_COS + C * DA // 2
N_C = C_SIN + C * DA // 2

PRODUCTS = [(0, 0), (0, 1), (1, 0), (1, 1), (0, 2), (2, 0)]
K_MAX = 96
K_ALL = K_MAX + 3

MAX_GROUPS = []
for _qt in range(C):
    _n = {0: 8, 1: 4, 2: 2, 3: 2}[_qt]
    MAX_GROUPS += [(_qt, _h, _n) for _h in range(0, HA, _n)]
EXP_GROUPS = [(0, 0, 2), (0, 2, 2), (1, 0, 2), (1, 2, 2), (2, 0, 4), (3, 0, 4)]
P_OFF = [0, 512, 896, 1152]
P_LEN = 1280

DVE_STEPS = 186


def hybrid_block(nc, x, weights, vectors, consts, consts_bf, scratch, out):
    with ExitStack() as ctx:
        def sb(name, shape, dt=F32):
            return ctx.enter_context(nc.sbuf_tensor(name, shape, dt))

        def sem(name):
            return ctx.enter_context(nc.semaphore(name))

        ps = ctx.enter_context(nc.psum_tensor("ps", [P, 8, 512], F32))

        w = sb("w", [P, N_W])
        vec = sb("vec", [P, N_V])
        cst = sb("cst", [P, N_C])
        cbf = sb("cbf", [P, 3 * P], BF16)
        sgn = sb("sgn", [P, D])
        sgn_neg = sb("sgn_neg", [P, D])
        half = sb("half", [P, C])
        x0 = sb("x0", [P, C, D])
        x1 = sb("x1", [P, C, D])
        x2 = sb("x2", [P, C, D])
        x3 = sb("x3", [P, C, D])
        x4 = sb("x4", [P, C, D])
        xn = sb("xn", [P, C, D])
        xnt = sb("xnt", [P, T])
        stats = sb("stats", [P, C, 6])
        mv = sb("mv", [P, 5, C])
        mean = sb("mean", [P, C])
        ve = sb("ve", [P, C])
        rstd = sb("rstd", [P, C])
        eq = sb("eq", [P, 2, T])
        qT = sb("qT", [P, T])
        kT = sb("kT", [P, T])
        km_flat = sb("km_flat", [P, H * T])
        kM = km_flat[:, :].rearrange("p (h t) -> p h t", t=T)
        qkv = km_flat[:, 0:C * 3 * D].rearrange("p (c n) -> p c n", c=C)
        ro = km_flat[:, C * 3 * D:C * 3 * D + 2 * C * 2 * D].rearrange("p (n c h e) -> p n c h e", n=4, c=C, e=DA // 2)
        ek = sb("ek", [P, C, D])
        ktok = sb("ktok", [P, C, D])
        gates = sb("gates", [P, C, N_GATES])
        gin = sb("gin", [P, C, 2 * HJ])
        bneg = sb("bneg", [P, C, HJ])
        mmax = sb("mmax", [P, C, H])
        gex = sb("gex", [P, C, 2 * HJ + H])
        bln = sb("bln", [P, C, HJ])
        alog = sb("alog", [P, C, HJ])
        alogx = sb("alogx", [P, C, J, D])
        gsig = sb("gsig", [P, C, H])
        mixw = sb("mixw", [P, C, J, H])
        vg = sb("vg", [P, C, H, QUAD])
        work = sb("work", [P, 2 * 4 * P_LEN])
        ae = work[:, 0:2 * HJ * P].rearrange("p (a n t) -> p a n t", a=2, t=P)
        dec = work[:, 2 * HJ * P:4 * HJ * P].rearrange("p (a n t) -> p a n t", a=2, t=P)
        am = work[:, 4 * HJ * P:5 * HJ * P].rearrange("p (h j t) -> p h j t", j=J, t=P)
        pT = work[:, :].rearrange("p (a i n) -> p a i n", a=2, n=P_LEN)
        gm = sb("gm", [P, H, P])
        pdec = sb("pdec", [P, J, P])
        qp = sb("qp", [P, J, P])
        kd = sb("kd", [P, J, D])
        sadd = sb("sadd", [P, J, H, DH + 1])
        state = sb("state", [P, 2, J, H, QUAD])
        yT = sb("yT", [P, 2, J, P])
        rec = sb("rec", [P, HJ])
        ytmp = sb("ytmp", [P, HJ, DH])
        ytok = sb("ytok", [P, C, D])
        ynt = sb("ynt", [P, T])
        hres = sb("hres", [P, C, D])
        qr = sb("qr", [P, C, 2 * D])
        parts = sb("parts", [P, 3, 2 * T], BF16)
        resid = sb("resid", [P, 2 * T])
        qs = sb("qs", [P, HA, T], BF16)
        ks = sb("ks", [P, HA, T], BF16)
        va = sb("va", [P, C, HA, QUAD])
        mrow = sb("mrow", [P, C, HA])
        mres = sb("mres", [P, 2, C, HA])
        mparts = sb("mparts", [P, C, P], BF16)
        mp = mparts[:, :, 0:3 * HA].rearrange("p c (n h) -> p c n h", n=3)
        mT = sb("mT", [P, T], BF16)
        oT = sb("oT", [P, 4, T])
        crec = sb("crec", [P, C * HA])
        ctxt = sb("ctxt", [P, C, D])
        cT = sb("cT", [P, T])

        loaded = sem("loaded")
        x_in = sem("x_in")
        setup = sem("setup")
        sign_ready = sem("sign_ready")
        dve_step = sem("dve_step")
        var_ready = sem("var_ready")
        rstd_ready = sem("rstd_ready")
        xn_ready = sem("xn_ready")
        xnt_ps = sem("xnt_ps")
        xnt_ready = sem("xnt_ready")
        tok_ps = sem("tok_ps")
        qk_ps = sem("qk_ps")
        elu_exp = sem("elu_exp")
        gates_in = sem("gates_in")
        gates_abs = sem("gates_abs")
        gates_exp = sem("gates_exp")
        log_ready = sem("log_ready")
        qk_ready = sem("qk_ready")
        vg_ready = sem("vg_ready")
        ae_pool = sem("ae_pool")
        ae_dve = sem("ae_dve")
        e_ps = sem("e_ps")
        g_ps = sem("g_ps")
        pre_ps = sem("pre_ps")
        dec_ready = sem("dec_ready")
        pdec_ready = sem("pdec_ready")
        kd_ready = sem("kd_ready")
        gm_ready = sem("gm_ready")
        am_ready = sem("am_ready")
        su_ps = sem("su_ps")
        state_ready = sem("state_ready")
        y_ps = sem("y_ps")
        y_sb = sem("y_sb")
        yt_ps = sem("yt_ps")
        y_ready = sem("y_ready")
        ynt_ps = sem("ynt_ps")
        ynt_ready = sem("ynt_ready")
        out_ps = sem("out_ps")
        x1_ready = sem("x1_ready")
        ffn_ps = sem("ffn_ps")
        qkv_ps = sem("qkv_ps")
        rope_ready = sem("rope_ready")
        qkt_ps = sem("qkt_ps")
        part0 = sem("part0")
        res1 = sem("res1")
        part1 = sem("part1")
        part2 = sem("part2")
        spilled = sem("spilled")
        stacked = sem("stacked")
        max_ps = sem("max_ps")
        max_done = sem("max_done")
        mparts_ready = sem("mparts_ready")
        mt_ps = sem("mt_ps")
        mt_ready = sem("mt_ready")
        mstacked = sem("mstacked")
        sc_ps = sem("sc_ps")
        probs_ready = sem("probs_ready")
        va_ready = sem("va_ready")
        pv_ps = sem("pv_ps")
        ot_ready = sem("ot_ready")
        ctx_ps = sem("ctx_ps")
        ctx_ready = sem("ctx_ready")
        ct_ps = sem("ct_ps")
        ct_ready = sem("ct_ready")
        proj_ps = sem("proj_ps")
        x4_ready = sem("x4_ready")
        stored = sem("stored")
        out_free = sem("out_free")

        ident = cst[:, C_ID:C_ID + P]
        tri = cst[:, C_TRI:C_TRI + P]
        after = cst[:, C_AFTER:C_AFTER + P]
        headmask = cst[:, C_HEAD:C_HEAD + H]
        slope = cst[:, C_SLOPE:C_SLOPE + HJ]
        ident_bf = cbf[:, 0:P]
        future_qk = cbf[:, P:2 * P]
        future_kq = cbf[:, 2 * P:3 * P]
        NG = len(MAX_GROUPS)
        NE = 4 * len(EXP_GROUPS)

        def tiles(ap):
            return ap.rearrange("o (c p) d -> p (o c) d", p=P)

        block = ctx.enter_context(nc.Block())

        @block.sync
        def _(sp):
            sp.dma_start(cst[:, :], consts).then_inc(loaded, 16)
            sp.dma_start(x0[:, :, :], tiles(x[0:1])).then_inc(x_in, 16)
            sp.dma_start(w[:, :], weights).then_inc(loaded, 16)
            sp.dma_start(vec[:, :], vectors.partition_broadcast(P)).then_inc(loaded, 16)
            sp.dma_start(cbf[:, :], consts_bf).then_inc(loaded, 16)
            sp.sem_inc(out_free, 1)

            def row(b, last):
                sp.wait_ge(part0, b + 1)
                sp.dma_start(scratch[0], parts[:, 0, :]).then_inc(spilled, 16)
                sp.wait_ge(part1, b + 1)
                sp.dma_start(scratch[1], parts[:, 1, :]).then_inc(spilled, 16)
                sp.wait_ge(part2, b + 1)
                sp.dma_start(scratch[2], parts[:, 2, :]).then_inc(spilled, 16)
                sp.wait_ge(spilled, b * 48 + 48)
                for n, (pq, pk) in enumerate(PRODUCTS):
                    for side, (dst, part) in enumerate(((qs, pq), (ks, pk))):
                        src = scratch[part, :, side * T:(side + 1) * T].rearrange("(h d) t -> d h t", d=DA)
                        sp.dma_start(dst[n * DA:(n + 1) * DA, :, :], src).then_inc(stacked, 16)
                if not last:
                    sp.wait_ge(x1_ready, b + 1)
                    sp.dma_start(x0[:, :, :], tiles(x[bass.ds(b + 1, 1)])).then_inc(x_in, 16)
                sp.wait_ge(mt_ready, b + 1)
                for part in range(3):
                    sp.dma_start(qs[K_MAX + part:K_MAX + part + 1, :, :],
                                 mT[part * HA:(part + 1) * HA, :]).then_inc(mstacked, 16)
                sp.wait_ge(x4_ready, b + 1)
                sp.dma_start(tiles(out[bass.ds(b, 1)]), x4[:, :, :]).then_inc(stored, 16)
                sp.wait_ge(stored, b * 16 + 16)
                sp.sem_inc(out_free, 1)

            with sp.Fori(0, B - 1) as b:
                row(b, False)
            row(B - 1, True)

        @block.gpsimd
        def _(pool):
            pool.memset(half[:, :], -0.5).then_inc(setup, 1)
            pool.memset(vg[:, :, :, :], 0.0).then_inc(setup, 1)
            pool.memset(va[:, :, :, :], 0.0).then_inc(setup, 1)
            pool.memset(state[:, :, :, :, :], 0.0).then_inc(setup, 1)
            pool.memset(qs[:, :, :], 0.0).then_inc(setup, 1)
            pool.memset(ks[:, :, :], 0.0).then_inc(setup, 1)
            pool.memset(mparts[:, :, :], 0.0).then_inc(setup, 1)
            pool.wait_ge(setup, 7)
            pool.memset(va[:, :, :, DA:DA + 1], 1.0).then_inc(setup, 1)
            pool.wait_ge(setup, 8)
            pool.memset(ks[K_MAX:K_ALL, :, :], 1.0).then_inc(setup, 1)
            pool.wait_ge(setup, 9)
            pool.wait_ge(loaded, 64)

            with pool.Fori(0, B) as b:
                def rsqrt(k):
                    pool.wait_ge(var_ready, b * 5 + k)
                    pool.tensor_tensor(rstd[:, :], ve[:, :], half[:, :], ALU.pow).then_inc(rstd_ready, 1)

                rsqrt(1)
                for c in range(C):
                    if c == 0:
                        pool.wait_ge(log_ready, b + 1)
                    if c >= 2:
                        pool.wait_ge(e_ps, b * C + c - 1)
                    pool.tensor_tensor(
                        ae[:, c % 2, 0:H, :], alog[:, c, 0:H].unsqueeze(2).broadcast_to([P, H, P]),
                        tri.unsqueeze(1).broadcast_to([P, H, P]), ALU.mult).then_inc(ae_pool, 1)
                for k in range(2, 6):
                    rsqrt(k)

        @block.scalar
        def _(act):
            act.wait_ge(loaded, 64)
            with act.Fori(0, B) as b:
                def transposed(k):
                    act.wait_ge(xnt_ps, b * 4 + k)
                    act.activation(xnt[:, :], ps[:, 0, :], ACT.Copy).then_inc(xnt_ready, 1)

                transposed(1)
                act.wait_ge(tok_ps, b + 1)
                act.activation(ek[:, :, :], ps[:, 4:8, 0:D], ACT.Exp).then_inc(elu_exp, 1)
                act.wait_ge(gates_in, b + 1)
                act.activation(gex[:, :, 0:2 * HJ], gin[:, :, :], ACT.Exp).then_inc(gates_abs, 1)
                act.activation(gex[:, :, 2 * HJ:], gates[:, :, 2 * HJ:], ACT.Exp, scale=-1.0).then_inc(gates_exp, 1)
                act.wait_ge(gates_abs, b + 1)
                act.activation(bln[:, :, :], gex[:, :, 0:HJ], ACT.Ln, bias=1.0).then_inc(gates_exp, 1)
                for n in range(2):
                    act.wait_ge(qk_ps, b * 2 + n + 1)
                    act.activation(eq[:, n, :], ps[:, 1 + n, :], ACT.Exp).then_inc(elu_exp, 1)

                def decays(c):
                    act.wait_ge(e_ps, b * C + c + 1)
                    if c >= 2:
                        act.wait_ge(am_ready, b * C + c - 1)
                    act.activation(dec[:, c % 2, :, :], ps[:, 0:4, :], ACT.Exp).then_inc(dec_ready, 1)

                def prefix(c):
                    act.wait_ge(pre_ps, b * C + c + 1)
                    if c >= 1:
                        act.wait_ge(am_ready, b * C + c)
                    act.activation(pdec[:, :, :], ps[:, 6, 0:J * P], ACT.Exp).then_inc(pdec_ready, 1)

                decays(0)
                prefix(0)
                for c in range(C):
                    if c + 1 < C:
                        decays(c + 1)
                    act.wait_ge(y_ps, b * C + c + 1)
                    act.activation(yT[:, :, :, :], ps[:, 7, :], ACT.Copy).then_inc(y_sb, 1)
                    if c + 1 < C:
                        prefix(c + 1)
                act.wait_ge(ynt_ps, b + 1)
                act.activation(ynt[:, :], ps[:, 0, :], ACT.Copy).then_inc(ynt_ready, 1)
                transposed(2)
                transposed(3)
                act.wait_ge(qkt_ps, b + 1)
                act.activation(parts[:, 0, :], ps[:, 0:2, :], ACT.Copy).then_inc(part0, 1)
                act.wait_ge(res1, b + 1)
                act.activation(parts[:, 1, :], resid[:, :], ACT.Copy).then_inc(part1, 1)
                act.wait_ge(mt_ps, b + 1)
                act.activation(mT[:, :], ps[:, 4, :].bitcast(BF16)[:, 0:T], ACT.Copy).then_inc(mt_ready, 1)
                n = 0
                for g in range(4):
                    if g >= 2:
                        act.wait_ge(pv_ps, b * 4 + g - 1)
                    for kt, c0, m in EXP_GROUPS:
                        bk = 2 * (n % 2)
                        width = T - kt * P
                        per = m * width // 512 if kt >= 2 else m
                        if kt < 2:
                            src = ps[:, bk:bk + m, 0:width]
                        else:
                            src = ps[:, bk:bk + per, :].rearrange("p a (m n) -> p (a m) n", n=width)
                        act.wait_ge(sc_ps, b * NE + n + 1)
                        act.activation(pT[:, g % 2, c0:c0 + m, P_OFF[kt]:P_OFF[kt] + width], src,
                                       ACT.Exp, scale=SCALE).then_inc(probs_ready, 1)
                        n += 1
                    if g >= 1:
                        act.wait_ge(pv_ps, b * 4 + g)
                        act.activation(oT[:, g - 1, :], ps[:, 4 + g - 1, :], ACT.Copy).then_inc(ot_ready, 1)
                act.wait_ge(pv_ps, b * 4 + 4)
                act.activation(oT[:, 3, :], ps[:, 7, :], ACT.Copy).then_inc(ot_ready, 1)
                act.wait_ge(ct_ps, b + 1)
                act.activation(cT[:, :], ps[:, 4, :], ACT.Copy).then_inc(ct_ready, 1)
                transposed(4)

        @block.tensor
        def _(pe):
            pe.wait_ge(loaded, 64)
            pe.wait_ge(setup, 9)
            pe.wait_ge(sign_ready, 1)
            with pe.Fori(0, B) as b:
                def turn(dst, src):
                    for c in range(C):
                        mm = pe.transpose(ps[:, dst, c * P:(c + 1) * P], src[:, c, :], ident)
                    return mm

                def xn_turn(k):
                    pe.wait_ge(xn_ready, b * 4 + k)
                    turn(0, xn).then_inc(xnt_ps, 1)
                    pe.wait_ge(xnt_ready, b * 4 + k)

                def project(src, col, dst):
                    for c in range(C):
                        mm = pe.matmul(ps[:, dst, c * D:(c + 1) * D], src[:, c * P:(c + 1) * P], col,
                                       start=True, stop=True)
                    return mm

                xn_turn(1)
                for c in range(C):
                    mm = pe.matmul(ps[:, 4 + c, 0:N_TOK], xnt[:, c * P:(c + 1) * P], w[:, W_K:W_K + N_TOK],
                                   start=True, stop=True)
                mm.then_inc(tok_ps, 1)
                pe.matmul(ps[:, 1, :], w[:, W_Q:W_Q + D], xnt[:, :], start=True, stop=True).then_inc(qk_ps, 1)
                pe.matmul(ps[:, 2, :], w[:, W_K:W_K + D], xnt[:, :], start=True, stop=True).then_inc(qk_ps, 1)

                def exponents(c):
                    pe.wait_ge(ae_pool, b * C + c + 1)
                    pe.wait_ge(ae_dve, b * C + c + 1)
                    if c == 0:
                        pe.wait_ge(qk_ready, b + 1)
                    else:
                        pe.wait_ge(dec_ready, b * C + c)
                    for n in range(4):
                        mm = pe.matmul(ps[:, n, :], after, ae[:, c % 2, 4 * n:4 * n + 4, :], start=True, stop=True)
                    mm.then_inc(e_ps, 1)

                def products(c):
                    if c == 0:
                        pe.wait_ge(vg_ready, b + 1)
                    else:
                        pe.wait_ge(gm_ready, b * C + c)
                    for h in range(H):
                        mm = pe.matmul(ps[:, 4 + h // 4, (h % 4) * P:(h % 4 + 1) * P],
                                       kM[:, h, c * P:(c + 1) * P], qT[:, c * P:(c + 1) * P],
                                       start=True, stop=True)
                    mm.then_inc(g_ps, 1)

                def prefix(c):
                    for j in range(J):
                        mm = pe.matmul(ps[:, 6, j * P:(j + 1) * P], alogx[:, c, j, :], tri, start=True, stop=True)
                    mm.then_inc(pre_ps, 1)

                exponents(0)
                products(0)
                prefix(0)
                for c in range(C):
                    if c + 1 < C:
                        exponents(c + 1)
                        products(c + 1)
                        pe.wait_ge(kd_ready, b * C + c + 1)
                        pe.wait_ge(pdec_ready, b * C + c + 1)
                        for j in range(J):
                            mm = pe.matmul(ps[:, 6, j * 136:(j + 1) * 136], kd[:, j, :], vg[:, c, :, 0:DH + 1],
                                           start=True, stop=True)
                        mm.then_inc(su_ps, 1)
                    pe.wait_ge(am_ready, b * C + c + 1)
                    if c >= 1:
                        pe.wait_ge(state_ready, b * 3 + c)
                        pe.wait_ge(y_ready, b * C + c)
                        for g in range(2):
                            for j in range(J):
                                pe.matmul(ps[:, 7, (2 * g + j) * P:(2 * g + j + 1) * P],
                                          state[:, c % 2, j, 4 * g:4 * g + 4, :], qp[:, j, :],
                                          start=(g == 0 and j == 0), stop=False, skip_group_check=True)
                    for g in range(2):
                        for i in range(4):
                            mm = pe.matmul(ps[QUAD * i:QUAD * i + QUAD, 7, 256 * g:256 * g + 256],
                                           vg[:, c, 4 * g + i, :], am[:, 4 * g + i, :, :],
                                           start=(c == 0 and g == 0), stop=True, skip_group_check=True,
                                           tile_position=(0, QUAD * i))
                    mm.then_inc(y_ps, 1)
                    if c + 1 < C:
                        pe.wait_ge(state_ready, b * 3 + c + 1)
                        prefix(c + 1)
                    pe.wait_ge(y_sb, b * C + c + 1)
                    for g in range(2):
                        for j in range(J):
                            mm = pe.transpose(ps[:, 7, (2 * g + j) * P:(2 * g + j + 1) * P], yT[:, g, j, :], ident)
                    mm.then_inc(yt_ps, 1)
                pe.wait_ge(y_ready, b * C + C)
                turn(0, ytok).then_inc(ynt_ps, 1)
                pe.wait_ge(ynt_ready, b + 1)
                project(ynt, w[:, W_OUT:W_OUT + D], 1).then_inc(out_ps, 1)
                xn_turn(2)
                project(xnt, sgn[:, :], 1).then_inc(ffn_ps, 1)
                xn_turn(3)
                for c in range(C):
                    mm = pe.matmul(ps[:, 4 + c, 0:3 * D], xnt[:, c * P:(c + 1) * P], w[:, W_QKV:W_QKV + 3 * D],
                                   start=True, stop=True)
                mm.then_inc(qkv_ps, 1)
                pe.wait_ge(rope_ready, b + 1)
                for side in range(2):
                    for c in range(C):
                        mm = pe.transpose(ps[:, side, c * P:(c + 1) * P], qr[:, c, side * D:(side + 1) * D], ident)
                mm.then_inc(qkt_ps, 1)
                pe.wait_ge(stacked, (b + 1) * (16 * 2 * len(PRODUCTS)))
                pe.wait_ge(part2, b + 1)
                for n, (qt, h0, m) in enumerate(MAX_GROUPS):
                    if n >= 2:
                        pe.wait_ge(max_done, b * NG + n - 1)
                    width = (qt + 1) * P
                    per = m // 2
                    for i in range(m):
                        o = ps[:, 2 * (n % 2) + i // per, (i % per) * width:(i % per + 1) * width]
                        pe.matmul(o, qs[0:K_MAX, h0 + i, qt * P:(qt + 1) * P], ks[0:K_MAX, h0 + i, 0:width],
                                  start=True, stop=False, skip_group_check=True)
                        mm = pe.matmul(o[:, qt * P:(qt + 1) * P], ident_bf, future_qk,
                                       start=False, stop=True, skip_group_check=True)
                    mm.then_inc(max_ps, 1)
                pe.wait_ge(mparts_ready, b + 1)
                for c in range(C):
                    mm = pe.transpose(ps[:, 4, :].bitcast(BF16)[:, c * P:(c + 1) * P],
                                      mparts[:, c, :], ident_bf)
                mm.then_inc(mt_ps, 1)
                pe.wait_ge(mstacked, b * 48 + 48)
                pe.wait_ge(va_ready, b + 1)

                def scores(n):
                    g, (kt, c0, m) = n // 6, EXP_GROUPS[n % 6]
                    if n >= 2:
                        pe.wait_ge(probs_ready, b * NE + n - 1)
                    width = T - kt * P
                    per = 512 // width if kt >= 2 else 1
                    for i in range(m):
                        h = 4 * g + c0 + i
                        o = ps[:, 2 * (n % 2) + i // per, (i % per) * width:(i % per + 1) * width]
                        pe.matmul(o, ks[0:K_ALL, h, kt * P:(kt + 1) * P], qs[0:K_ALL, h, kt * P:T],
                                  start=True, stop=False, skip_group_check=True)
                        mm = pe.matmul(o[:, 0:P], ident_bf, future_kq, start=False, stop=True, skip_group_check=True)
                    mm.then_inc(sc_ps, 1)

                def values(n):
                    g, (kt, c0, m) = n // 6, EXP_GROUPS[n % 6]
                    pe.wait_ge(probs_ready, b * NE + n + 1)
                    if n == 0:
                        pe.wait_ge(mt_ready, b + 1)
                    for i in range(m):
                        q = QUAD * (c0 + i)
                        mm = pe.matmul(ps[q:q + QUAD, 4 + g, kt * P:T], va[:, kt, 4 * g + c0 + i, :],
                                       pT[:, g % 2, c0 + i, P_OFF[kt]:P_OFF[kt] + T - kt * P],
                                       start=(kt == 0), stop=(kt == C - 1), skip_group_check=True,
                                       tile_position=(0, q))
                    if n % 6 == 5:
                        mm.then_inc(pv_ps, 1)

                scores(0)
                for n in range(NE):
                    if n + 1 < NE:
                        scores(n + 1)
                    values(n)
                pe.wait_ge(ot_ready, b * 4 + 4)
                for c in range(C):
                    for g in range(4):
                        mm = pe.transpose(ps[:, c, g * P:(g + 1) * P], oT[:, g, c * P:(c + 1) * P], ident)
                mm.then_inc(ctx_ps, 1)
                pe.wait_ge(ctx_ready, b + 1)
                turn(4, ctxt).then_inc(ct_ps, 1)
                pe.wait_ge(ct_ready, b + 1)
                project(cT, w[:, W_PROJ:W_PROJ + D], 5).then_inc(proj_ps, 1)
                xn_turn(4)
                project(xnt, sgn[:, :], 1).then_inc(ffn_ps, 1)

        @block.vector
        def _(dve):
            dve.wait_ge(loaded, 64)
            dve.tensor_scalar(sgn_neg[:, :], w[:, W_FFN:W_FFN + D], 0.0, None, ALU.is_lt).then_inc(dve_step, 1)
            dve.wait_ge(dve_step, 1)
            dve.scalar_tensor_tensor(sgn[:, :], w[:, W_FFN:W_FFN + D], 0.0, sgn_neg[:, :],
                                     ALU.is_gt, ALU.subtract).then_inc(sign_ready, 1)
            dve.wait_ge(setup, 9)

            with dve.Fori(0, B) as b:
                steps = [0]

                def step(ins):
                    steps[0] += 1
                    ins.then_inc(dve_step, 1)
                    dve.wait_ge(dve_step, b * DVE_STEPS + (1 + steps[0]))

                def counted(ins):
                    steps[0] += 1
                    ins.then_inc(dve_step, 1)

                def over_features(ap, n):
                    return ap.unsqueeze(2).broadcast_to([P, ap.shape[1], n])

                def row_vector(col):
                    return vec[:, col:col + D].unsqueeze(1).broadcast_to([P, C, D])

                def layernorm(src, k):
                    for c in range(C):
                        counted(dve.bn_stats(stats[:, c, :], src[:, c, :]))
                    dve.wait_ge(dve_step, b * DVE_STEPS + (1 + steps[0]))
                    m0, m1, v0, v1 = stats[:, :, 1], stats[:, :, 4], stats[:, :, 2], stats[:, :, 5]
                    counted(dve.tensor_tensor(mv[:, 0, :], m0, m1, ALU.add))
                    counted(dve.tensor_tensor(mv[:, 1, :], m0, m1, ALU.subtract))
                    step(dve.tensor_tensor(mv[:, 2, :], v0, v1, ALU.add))
                    counted(dve.tensor_scalar(mean[:, :], mv[:, 0, :], 0.5, None, ALU.mult))
                    counted(dve.scalar_tensor_tensor(mv[:, 3, :], mv[:, 1, :], 0.25, mv[:, 1, :], ALU.mult, ALU.mult))
                    step(dve.tensor_scalar(mv[:, 4, :], mv[:, 2, :], 1.0 / D, LN_EPS, ALU.mult, ALU.add))
                    dve.tensor_tensor(ve[:, :], mv[:, 3, :], mv[:, 4, :], ALU.add).then_inc(var_ready, 1)
                    dve.wait_ge(rstd_ready, b * 5 + k)
                    for c in range(C):
                        ins = dve.tensor_scalar(xn[:, c, :], src[:, c, :], mean[:, c:c + 1], rstd[:, c:c + 1],
                                                ALU.subtract, ALU.mult)
                        if c < C - 1:
                            counted(ins)
                    return ins

                dve.wait_ge(x_in, b * 16 + 16)
                layernorm(x0, 1).then_inc(xn_ready, 1)
                dve.wait_ge(elu_exp, b * 3 + 1)
                step(dve.tensor_tensor(gates[:, :, :], ps[:, 4:8, 2 * D:N_TOK],
                                       vec[:, V_GATES:V_GATES + N_GATES].unsqueeze(1)
                                       .broadcast_to([P, C, N_GATES]), ALU.add))
                beta = gates[:, :, 0:HJ]
                mix = gates[:, :, HJ:2 * HJ].rearrange("p c (h j) -> p c h j", j=J)
                counted(dve.tensor_scalar(bneg[:, :, :], beta, 0.0, None, ALU.min))
                step(dve.tensor_tensor(mmax[:, :, :], mix[:, :, :, 0], mix[:, :, :, 1], ALU.max))
                counted(dve.scalar_tensor_tensor(gin[:, :, 0:HJ], bneg[:, :, :], 2.0, beta, ALU.mult, ALU.subtract))
                dve.tensor_tensor(gin[:, :, HJ:].rearrange("p c (j h) -> p c j h", j=J),
                                  mix.rearrange("p c h j -> p c j h"),
                                  mmax[:, :, :].unsqueeze(2).broadcast_to([P, C, J, H]),
                                  ALU.subtract).then_inc(gates_in, 1)
                step(dve.tensor_scalar(ek[:, :, :], ek[:, :, :], 1.0, None, ALU.min))
                counted(dve.scalar_tensor_tensor(ktok[:, :, :], ps[:, 4:8, 0:D], 0.0, ek[:, :, :],
                                                 ALU.max, ALU.add))
                dve.wait_ge(gates_exp, b * 2 + 2)
                step(dve.tensor_tensor(bneg[:, :, :], bneg[:, :, :], bln[:, :, :], ALU.subtract))
                step(dve.tensor_tensor(bneg[:, :, :], bneg[:, :, :],
                                       slope.unsqueeze(1).broadcast_to([P, C, HJ]), ALU.subtract))
                step(dve.tensor_scalar(alog[:, :, :], bneg[:, :, :], BETA_CAP, None, ALU.min))
                for c in range(C):
                    ins = dve.tensor_copy(alogx[:, c, :, :].rearrange("p j (h d) -> p j h d", d=DH),
                                          alog[:, c, :].rearrange("p (h j) -> p j h", j=J)
                                          .unsqueeze(3).broadcast_to([P, J, H, DH]))
                    if c < C - 1:
                        counted(ins)
                ins.then_inc(log_ready, 1)

                def triangles(c):
                    if c >= 2:
                        dve.wait_ge(e_ps, b * C + c - 1)
                    for i in range(H, HJ):
                        ins = dve.tensor_scalar(ae[:, c % 2, i, :], tri, alog[:, c, i:i + 1], None, ALU.mult)
                        if i < HJ - 1:
                            counted(ins)
                    ins.then_inc(ae_dve, 1)

                triangles(0)
                counted(dve.tensor_scalar(gsig[:, :, :], gex[:, :, 2 * HJ:], 1.0, None, ALU.add))
                mexp = gex[:, :, HJ:2 * HJ].rearrange("p c (j h) -> p c j h", j=J)
                step(dve.tensor_tensor(mmax[:, :, :], mexp[:, :, 0, :], mexp[:, :, 1, :], ALU.add))
                counted(dve.reciprocal(gsig[:, :, :], gsig[:, :, :]))
                step(dve.reciprocal(mmax[:, :, :], mmax[:, :, :]))
                counted(dve.tensor_tensor(mixw[:, :, :, :], mexp,
                                          mmax[:, :, :].unsqueeze(2).broadcast_to([P, C, J, H]), ALU.mult))
                counted(dve.tensor_copy(vg[:, :, :, DH], gsig[:, :, :]))
                for c in range(C):
                    ins = dve.tensor_tensor(vg[:, c, :, 0:DH],
                                            ps[:, 4 + c, D:2 * D].rearrange("p (h d) -> p h d", d=DH),
                                            over_features(gsig[:, c, :], DH), ALU.mult)
                    if c < C - 1:
                        counted(ins)
                ins.then_inc(vg_ready, 1)
                for n, dst in enumerate((qT, kT)):
                    dve.wait_ge(elu_exp, b * 3 + 2 + n)
                    step(dve.tensor_scalar(eq[:, n, :], eq[:, n, :], 1.0, None, ALU.min))
                    step(dve.scalar_tensor_tensor(dst[:, :], ps[:, 1 + n, :], 0.0, eq[:, n, :], ALU.max, ALU.add))
                for h in range(H):
                    ins = dve.tensor_scalar(kM[:, h, :], kT[:, :], headmask[:, h:h + 1], None, ALU.mult)
                    if h < H - 1:
                        counted(ins)
                ins.then_inc(qk_ready, 1)

                for c in range(C):
                    if c + 1 < C:
                        triangles(c + 1)
                    dve.wait_ge(g_ps, b * C + c + 1)
                    dve.tensor_tensor(gm[:, :, :], ps[:, 4:6, :].rearrange("p a (h t) -> p (a h) t", t=P),
                                      tri.unsqueeze(1).broadcast_to([P, H, P]), ALU.mult).then_inc(gm_ready, 1)
                    dve.wait_ge(gm_ready, b * C + c + 1)
                    dve.wait_ge(dec_ready, b * C + c + 1)
                    dv = dec[:, c % 2, :, :].rearrange("p (h j) t -> p h j t", j=J)
                    for j in range(J):
                        ins = dve.tensor_tensor(kd[:, j, :].rearrange("p (h d) -> p h d", d=DH),
                                                ktok[:, c, :].rearrange("p (h d) -> p h d", d=DH),
                                                over_features(dv[:, :, j, P - 1], DH), ALU.mult)
                        if j == 0:
                            counted(ins)
                    ins.then_inc(kd_ready, 1)
                    counted(dve.tensor_tensor(am[:, :, :, :], dv,
                                              gm[:, :, :].unsqueeze(2).broadcast_to([P, H, J, P]), ALU.mult))
                    dve.wait_ge(pdec_ready, b * C + c + 1)
                    dve.tensor_tensor(qp[:, :, :], pdec[:, :, :],
                                      qT[:, c * P:(c + 1) * P].unsqueeze(1).broadcast_to([P, J, P]),
                                      ALU.mult).then_inc(am_ready, 1)
                    if c + 1 < C:
                        dve.wait_ge(su_ps, b * 3 + c + 1)
                        old, dst = (state[:, n % 2, :, :, 0:DH + 1] for n in (c, c + 1))
                        su = ps[:, 6, 0:J * 136].rearrange("p (j h e) -> p (j h) e", j=J, e=DH + 1)
                        hm = headmask.unsqueeze(2).broadcast_to([P, H, DH + 1])
                        for j in range(J):
                            o = dst[:, j] if c == 0 else sadd[:, j]
                            ins = dve.tensor_tensor(o, su[:, j * H:(j + 1) * H, :], hm, ALU.mult)
                            if c > 0:
                                counted(ins)
                            elif j == 0:
                                counted(ins)
                            else:
                                ins.then_inc(state_ready, 1)
                        if c > 0:
                            dve.wait_ge(dve_step, b * DVE_STEPS + (1 + steps[0]))
                            for j in range(J):
                                ins = dve.scalar_tensor_tensor(dst[:, j], old[:, j], pdec[:, j, P - 1:P],
                                                               sadd[:, j], ALU.mult, ALU.add)
                                if j == 0:
                                    counted(ins)
                            ins.then_inc(state_ready, 1)
                    dve.wait_ge(yt_ps, b * C + c + 1)
                    yv = ps[:, 7, :].rearrange("p (n e) -> p n e", e=QUAD)
                    step(dve.tensor_scalar(rec[:, :], yv[:, :, DH], DEN_EPS, None, ALU.add))
                    step(dve.reciprocal(rec[:, :], rec[:, :]))
                    step(dve.tensor_tensor(rec[:, :].rearrange("p (g j i) -> p g j i", g=2, j=J),
                                           rec[:, :].rearrange("p (g j i) -> p g j i", g=2, j=J),
                                           mixw[:, c, :, :].rearrange("p j (g i) -> p g j i", g=2), ALU.mult))
                    step(dve.tensor_tensor(ytmp[:, :, :], yv[:, :, 0:DH], over_features(rec[:, :], DH), ALU.mult))
                    yj = ytmp[:, :, :].rearrange("p (g j i) e -> p g j (i e)", g=2, j=J)
                    dve.tensor_tensor(ytok[:, c, :].rearrange("p (g n) -> p g n", g=2), yj[:, :, 0, :],
                                      yj[:, :, 1, :], ALU.add).then_inc(y_ready, 1)

                dve.wait_ge(out_ps, b + 1)
                step(dve.tensor_tensor(hres[:, :, :], ps[:, 1, :].rearrange("p (c d) -> p c d", d=D),
                                       xn[:, :, :], ALU.add))
                step(dve.tensor_tensor(hres[:, :, :], hres[:, :, :], row_vector(V_BOUT), ALU.add))
                step(layernorm(hres, 2))
                step(dve.tensor_tensor(hres[:, :, :], xn[:, :, :], row_vector(V_LNG), ALU.mult))
                step(dve.tensor_tensor(hres[:, :, :], hres[:, :, :], row_vector(V_LNB), ALU.add))
                dve.tensor_tensor(x1[:, :, :], hres[:, :, :], x0[:, :, :], ALU.add).then_inc(x1_ready, 1)
                dve.wait_ge(x1_ready, b + 1)
                layernorm(x1, 3).then_inc(xn_ready, 1)
                dve.wait_ge(ffn_ps, b * 2 + 1)
                step(dve.tensor_tensor(x2[:, :, :], ps[:, 1, :].rearrange("p (c d) -> p c d", d=D),
                                       x1[:, :, :], ALU.add))
                layernorm(x2, 4).then_inc(xn_ready, 1)
                dve.wait_ge(qkv_ps, b + 1)
                step(dve.tensor_tensor(qkv[:, :, :], ps[:, 4:8, 0:3 * D],
                                       vec[:, V_QKV:V_QKV + 3 * D].unsqueeze(1).broadcast_to([P, C, 3 * D]),
                                       ALU.add))
                for c in range(C):
                    xa = qkv[:, c, 0:2 * D].rearrange("p (h e) -> p h e", e=DA)
                    lo, hi = xa[:, :, 0:DA // 2], xa[:, :, DA // 2:]
                    cos = cst[:, C_COS + 4 * c:C_COS + 4 * c + 4].unsqueeze(1).broadcast_to([P, 2 * HA, DA // 2])
                    sin = cst[:, C_SIN + 4 * c:C_SIN + 4 * c + 4].unsqueeze(1).broadcast_to([P, 2 * HA, DA // 2])
                    counted(dve.tensor_tensor(ro[:, 0, c], lo, cos, ALU.mult))
                    counted(dve.tensor_tensor(ro[:, 1, c], hi, sin, ALU.mult))
                    counted(dve.tensor_tensor(ro[:, 2, c], hi, cos, ALU.mult))
                    counted(dve.tensor_tensor(ro[:, 3, c], lo, sin, ALU.mult))
                dve.wait_ge(dve_step, b * DVE_STEPS + (1 + steps[0]))
                xr = qr[:, :, :].rearrange("p c (h e) -> p (c h) e", e=DA)
                rv = ro.rearrange("p n c h e -> p n (c h) e")
                counted(dve.tensor_tensor(xr[:, :, 0:DA // 2], rv[:, 0], rv[:, 1], ALU.subtract))
                dve.tensor_tensor(xr[:, :, DA // 2:], rv[:, 2], rv[:, 3], ALU.add).then_inc(rope_ready, 1)
                dve.tensor_copy(va[:, :, :, 0:DA],
                                qkv[:, :, 2 * D:].rearrange("p c (h e) -> p c h e", e=DA)).then_inc(va_ready, 1)
                dve.wait_ge(part0, b + 1)
                dve.tensor_tensor(resid[:, :].rearrange("p (a t) -> p a t", a=2), ps[:, 0:2, :],
                                  parts[:, 0, :].rearrange("p (a t) -> p a t", a=2), ALU.subtract).then_inc(res1, 1)
                dve.wait_ge(part1, b + 1)
                dve.wait_ge(res1, b + 1)
                dve.tensor_tensor(parts[:, 2, :], resid[:, :], parts[:, 1, :], ALU.subtract).then_inc(part2, 1)
                for n, (qt, h0, m) in enumerate(MAX_GROUPS):
                    dve.wait_ge(max_ps, b * NG + n + 1)
                    width = (qt + 1) * P
                    bk = 2 * (n % 2)
                    if qt >= 2:
                        src = ps[:, bk:bk + 2, 0:width]
                    else:
                        src = ps[:, bk:bk + 2, :].rearrange("p a (m k) -> p (a m) k", k=width)
                    dve.tensor_reduce(mrow[:, qt, h0:h0 + m], src, AX.X, ALU.max).then_inc(max_done, 1)
                dve.wait_ge(max_done, b * NG + NG)
                step(dve.tensor_scalar(mp[:, :, 0, :], mrow[:, :, :], -1.0, None, ALU.mult))
                step(dve.scalar_tensor_tensor(mres[:, 0], mrow[:, :, :], -1.0, mp[:, :, 0, :],
                                              ALU.mult, ALU.subtract))
                step(dve.tensor_copy(mp[:, :, 1, :], mres[:, 0]))
                dve.tensor_tensor(mp[:, :, 2, :], mres[:, 0], mp[:, :, 1, :],
                                  ALU.subtract).then_inc(mparts_ready, 1)
                dve.wait_ge(ctx_ps, b + 1)
                cv = ps[:, 0:4, :].rearrange("p c (h e) -> p (c h) e", e=QUAD)
                step(dve.reciprocal(crec[:, :], cv[:, :, DA]))
                dve.tensor_tensor(ctxt[:, :, :].rearrange("p c (h e) -> p (c h) e", e=DA), cv[:, :, 0:DA],
                                  over_features(crec[:, :], DA), ALU.mult).then_inc(ctx_ready, 1)
                dve.wait_ge(proj_ps, b + 1)
                step(dve.tensor_tensor(hres[:, :, :], ps[:, 5, :].rearrange("p (c d) -> p c d", d=D),
                                       x2[:, :, :], ALU.add))
                step(dve.tensor_tensor(x3[:, :, :], hres[:, :, :], row_vector(V_PROJ), ALU.add))
                layernorm(x3, 5).then_inc(xn_ready, 1)
                dve.wait_ge(ffn_ps, b * 2 + 2)
                dve.wait_ge(out_free, b + 1)
                dve.tensor_tensor(x4[:, :, :], ps[:, 1, :].rearrange("p (c d) -> p c d", d=D),
                                  x3[:, :, :], ALU.add).then_inc(x4_ready, 1)
                dve.wait_ge(x4_ready, b + 1)
                assert steps[0] == DVE_STEPS, steps[0]


def _alibi_slopes():
    start = 2.0 ** (-2.0 ** (-(math.log2(H) - 3)))
    return np.array([start * start ** i for i in range(H)], np.float32)


def _constants():
    i = np.arange(P)
    c = np.zeros((P, N_C), np.float32)
    c[:, C_ID:C_ID + P] = np.eye(P)
    c[:, C_TRI:C_TRI + P] = i[:, None] <= i[None, :]
    c[:, C_AFTER:C_AFTER + P] = i[:, None] > i[None, :]
    c[:, C_HEAD:C_HEAD + H] = (i // DH)[:, None] == np.arange(H)[None, :]
    c[:, C_SLOPE:C_SLOPE + HJ] = np.repeat(_alibi_slopes(), J)[None, :]
    inv = (1.0 / np.float32(10000.0) ** (np.arange(0, DA, 2, dtype=np.float32) / np.float32(DA))).astype(np.float32)
    ang = (np.arange(T, dtype=np.float32)[:, None] * inv[None, :]).astype(np.float32)
    for t in range(C):
        c[:, C_COS + 4 * t:C_COS + 4 * t + 4] = np.cos(ang[t * P:(t + 1) * P])
        c[:, C_SIN + 4 * t:C_SIN + 4 * t + 4] = np.sin(ang[t * P:(t + 1) * P])
    f = np.zeros((P, 3 * P), np.float32)
    f[:, 0:P] = np.eye(P)
    f[:, P:2 * P] = np.where(i[None, :] > i[:, None], NEG, 0.0)
    f[:, 2 * P:] = np.where(i[:, None] > i[None, :], NEG, 0.0)
    return c, f


def kernel(**inputs):
    import concourse.bacc as _bacc
    from concourse.bass_utils import run_bass_kernel_spmd as _run

    g = {k: np.asarray(v) for k, v in inputs.items()}
    a, c = "L0_attn_a_", "L0_attn_b_"
    weights = np.ascontiguousarray(np.concatenate(
        [g[a + "Wq"].T, g[a + "Wk"].T, g[a + "Wv"].T, g[a + "Wbeta"].T, g[a + "Wmix"].T, g[a + "Wgate"].T,
         g[a + "Wout"].T, g["L0_ffn_weight"].T, g[c + "qkv_w"].T, g[c + "proj_w"].T], axis=1))
    vectors = np.concatenate([g[a + "bbeta"], g[a + "bmix"], g[a + "bgate"], g[a + "bout"], g[a + "ln_g"],
                              g[a + "ln_b"], g[c + "qkv_b"], g[c + "proj_b"]])
    cf, cb = _constants()
    arrays = {"x": np.ascontiguousarray(g[a + "x"]), "weights": weights, "vectors": vectors, "consts": cf,
              "consts_bf": cb.astype(mybir.dt.np(BF16))}
    nc = _bacc.Bacc("TRN2", target_bir_lowering=False, num_devices=1)
    args = {n: nc.dram_tensor(n, v.shape, mybir.dt.from_np(v.dtype), kind="ExternalInput").ap()
            for n, v in arrays.items()}
    scratch = nc.dram_tensor("scratch", (3, P, 2 * T), BF16).ap()
    out = nc.dram_tensor("out", (B, T, D), F32, kind="ExternalOutput").ap()
    hybrid_block(nc, args["x"], args["weights"], args["vectors"], args["consts"], args["consts_bf"], scratch, out)
    r = _run(nc, [arrays], core_ids=[0])
    return r.results[0]["out"]
```

```python
import math
from contextlib import ExitStack

import numpy as np

import concourse.bass as bass
from concourse import mybir

F32 = mybir.dt.float32
BF16 = mybir.dt.bfloat16
ALU = mybir.AluOpType
ACT = mybir.ActivationFunctionType
AX = mybir.AxisListType

B, T, D = 8, 512, 128
P = 128
C = T // P
H, J, DH = 8, 2, 16
HJ = H * J
QUAD = 32
HA, DA = 16, 8
LN_EPS = 1e-5
DEN_EPS = 1e-6
BETA_CAP = math.log(0.9999)
SCALE = 1.0 / math.sqrt(DA)
NEG = -3.0e38

W_Q, W_K, W_V = 0, 128, 256
W_GATES = 384
N_GATES = 2 * HJ + H
W_OUT = W_GATES + N_GATES
W_FFN = W_OUT + D
W_QKV = W_FFN + D
W_PROJ = W_QKV + 3 * D
N_W = W_PROJ + D
N_TOK = 2 * D + N_GATES

V_GATES, V_BOUT, V_LNG, V_LNB, V_QKV = 0, 40, 168, 296, 424
V_PROJ = V_QKV + 3 * D
N_V = V_PROJ + D

C_ID, C_TRI, C_AFTER = 0, 128, 256
C_HEAD = 384
C_SLOPE = C_HEAD + H
C_COS = C_SLOPE + HJ
C_SIN = C_COS + C * DA // 2
N_C = C_SIN + C * DA // 2

PRODUCTS = [(0, 0), (0, 1), (1, 0), (1, 1), (0, 2), (2, 0)]
K_MAX = 96
K_ALL = K_MAX + 3

MAX_GROUPS = [(qt, h, n) for qt, n in enumerate((8, 4, 2, 2)) for h in range(0, HA, n)]
NG = len(MAX_GROUPS)
EXP_GROUPS = [(kt, c0, n) for kt, n in enumerate((1, 1, 2, 4)) for c0 in range(0, 4, n)]
NE = len(EXP_GROUPS)
P_OFF = [0, 512, 896, 1152]
P_LEN = 1280

FRONT_STEPS = 112
BACK_STEPS = 18

FRONT_PHASES = 42


def at_front(phase):
    return 100.0 * phase / FRONT_PHASES


def at_chunk(c, s):
    return at_front(9 + 4 * (c + 1) + s)


def at_post(n):
    return at_front(29 + n)


def at_max(n):
    return 10 + 32.0 * n / NG


def at_minus(n):
    return 42 + n


def at_exp(n):
    return 47 + 37.0 * n / (4 * NE)


def at_tail(n):
    return 85 + 1.5 * n


def interleave(*rows):
    due = [[next(r), i, r] for i, r in enumerate(rows)]
    while due:
        first = min(due, key=lambda d: d[:2])
        place = next(first[2], None)
        if place is None:
            due.remove(first)
        else:
            assert place >= first[0], (place, first[0])
            first[0] = place


def hybrid_block(nc, x, weights, vectors, consts, consts_bf, scratch, out):
    with ExitStack() as ctx:
        def sb(name, shape, dt=F32):
            return ctx.enter_context(nc.sbuf_tensor(name, shape, dt))

        def sem(name):
            return ctx.enter_context(nc.semaphore(name))

        ps = ctx.enter_context(nc.psum_tensor("ps", [P, 8, 512], F32))

        w = sb("w", [P, N_W])
        vec = sb("vec", [P, N_V])
        cst = sb("cst", [P, N_C])
        cbf = sb("cbf", [P, 3 * P], BF16)
        sgn = sb("sgn", [P, D])
        sgn_neg = sb("sgn_neg", [P, D])
        half = sb("half", [P, C])
        x0 = sb("x0", [P, C, D])
        x1 = sb("x1", [P, C, D])
        x2 = sb("x2", [P, C, D])
        x2b = sb("x2b", [P, C, D])
        x3 = sb("x3", [P, C, D])
        x4 = sb("x4", [P, C, D])

        class Norm:

            def __init__(self, side):
                self.xn = sb(side + "_xn", [P, C, D])
                self.xnt = sb(side + "_xnt", [P, T])
                self.stats = sb(side + "_stats", [P, C, 6])
                self.mv = sb(side + "_mv", [P, 5, C])
                self.mean = sb(side + "_mean", [P, C])
                self.ve = sb(side + "_ve", [P, C])
                self.rstd = sb(side + "_rstd", [P, C])

        fn, bn = Norm("front"), Norm("back")
        qT = sb("qT", [P, T])
        kT = sb("kT", [P, T])
        km_flat = sb("km_flat", [P, H * T])
        kM = km_flat[:, :].rearrange("p (h t) -> p h t", t=T)
        qkv = km_flat[:, 0:C * 3 * D].rearrange("p (c n) -> p c n", c=C)
        ro = km_flat[:, C * 3 * D:C * 3 * D + 2 * C * 2 * D].rearrange("p (n c h e) -> p n c h e", n=4, c=C, e=DA // 2)
        ktok = sb("ktok", [P, C, D])
        gates = sb("gates", [P, C, N_GATES])
        gin = sb("gin", [P, C, 2 * HJ])
        bneg = sb("bneg", [P, C, HJ])
        mmax = sb("mmax", [P, C, H])
        gex = sb("gex", [P, C, 2 * HJ + H])
        bln = sb("bln", [P, C, HJ])
        alog = sb("alog", [P, C, HJ])
        alogx = sb("alogx", [P, C, J, D])
        gsig = sb("gsig", [P, C, H])
        mixw = sb("mixw", [P, C, J, H])
        vg = sb("vg", [P, C, H, QUAD])
        ae = sb("ae", [P, 2, HJ, P])
        dec = sb("dec", [P, 2, HJ, P])
        gm = sb("gm", [P, H, P])
        am = sb("am", [P, H, J, P])
        pdec = sb("pdec", [P, J, P])
        qp = sb("qp", [P, J, P])
        kd = sb("kd", [P, J, D])
        sadd = sb("sadd", [P, J, H, DH + 1])
        state = sb("state", [P, 2, J, H, QUAD])
        yT = sb("yT", [P, 2, J, P])
        rec = sb("rec", [P, HJ])
        ytmp = sb("ytmp", [P, HJ, DH])
        ytok = sb("ytok", [P, C, D])
        ynt = yT[:, :, :, :].rearrange("p g j t -> p (g j t)")
        hres = sb("hres", [P, C, D])
        ek = hres
        qr = sb("qr", [P, C, 2 * D])
        eq = qr[:, :, :].rearrange("p (n c) d -> p n (c d)", n=2)
        resid = qr[:, :, :].rearrange("p c n -> p (c n)")
        parts = sb("parts", [P, 3, 2 * T], BF16)
        qs = sb("qs", [P, HA, T], BF16)
        ks = sb("ks", [P, HA, T], BF16)
        va = sb("va", [P, C, HA, QUAD])
        mrow = sb("mrow", [P, C, HA])
        mres = sb("mres", [P, C, HA])
        mparts = sb("mparts", [P, C, P], BF16)
        mp = mparts[:, :, 0:3 * HA].rearrange("p c (n h) -> p c n h", n=3)
        mT = sb("mT", [P, T], BF16)
        pT = sb("pT", [P, 4, P_LEN])
        oT = sb("oT", [P, 4, T])
        crec = sb("crec", [P, C * HA])
        cT = oT[:, 0, :]
        ctxt = oT[:, 1, :].rearrange("p (c d) -> p c d", d=D)

        loaded = sem("loaded")
        x_in = sem("x_in")
        setup = sem("setup")
        sign_ready = sem("sign_ready")
        front_step = sem("front_step")
        pool_step = sem("pool_step")
        var_ready = sem("var_ready")
        rstd_ready = sem("rstd_ready")
        xn_ready = sem("xn_ready")
        xnt_ps = sem("xnt_ps")
        xnt_ready = sem("xnt_ready")
        gates_ps = sem("gates_ps")
        kv_ps = sem("kv_ps")
        qk_ps = sem("qk_ps")
        elu_exp = sem("elu_exp")
        gates_in = sem("gates_in")
        gates_abs = sem("gates_abs")
        gates_exp = sem("gates_exp")
        log_ready = sem("log_ready")
        qk_ready = sem("qk_ready")
        vg_ready = sem("vg_ready")
        ae_ready = sem("ae_ready")
        e_ps = sem("e_ps")
        dec_ready = sem("dec_ready")
        pre_ps = sem("pre_ps")
        pdec_ready = sem("pdec_ready")
        g_ps = sem("g_ps")
        gm_ready = sem("gm_ready")
        kd_ready = sem("kd_ready")
        qp_ready = sem("qp_ready")
        am_dve = sem("am_dve")
        am_pool = sem("am_pool")
        su_ps = sem("su_ps")
        state_ready = sem("state_ready")
        y_ps = sem("y_ps")
        y_sb = sem("y_sb")
        yt_ps = sem("yt_ps")
        y_ready = sem("y_ready")
        ynt_ps = sem("ynt_ps")
        ynt_ready = sem("ynt_ready")
        out_ps = sem("out_ps")
        hn_ready = sem("hn_ready")
        x1_ready = sem("x1_ready")
        ffn_ps = sem("ffn_ps")
        x2_ready = sem("x2_ready")
        qkv_ps = sem("qkv_ps")
        qkv_ready = sem("qkv_ready")
        rope_ready = sem("rope_ready")
        qkt_ps = sem("qkt_ps")
        part0 = sem("part0")
        res1 = sem("res1")
        part1 = sem("part1")
        part2 = sem("part2")
        va_ready = sem("va_ready")
        spilled = sem("spilled")
        back_step = sem("back_step")
        x2b_ready = sem("x2b_ready")
        stacked = sem("stacked")
        max_ps = sem("max_ps")
        max_done = sem("max_done")
        mparts_ready = sem("mparts_ready")
        mt_ps = sem("mt_ps")
        mt_ready = sem("mt_ready")
        mstacked = sem("mstacked")
        sc_ps = sem("sc_ps")
        probs_ready = sem("probs_ready")
        pv_ps = sem("pv_ps")
        ot_ready = sem("ot_ready")
        ctx_ps = sem("ctx_ps")
        ctx_ready = sem("ctx_ready")
        ct_ps = sem("ct_ps")
        ct_ready = sem("ct_ready")
        proj_ps = sem("proj_ps")
        var_back = sem("var_back")
        rstd_back = sem("rstd_back")
        xn_back = sem("xn_back")
        xnt_ps_back = sem("xnt_ps_back")
        xnt_back = sem("xnt_back")
        ffn_back = sem("ffn_back")
        x4_ready = sem("x4_ready")
        stored = sem("stored")
        out_free = sem("out_free")

        ident = cst[:, C_ID:C_ID + P]
        tri = cst[:, C_TRI:C_TRI + P]
        after = cst[:, C_AFTER:C_AFTER + P]
        headmask = cst[:, C_HEAD:C_HEAD + H]
        slope = cst[:, C_SLOPE:C_SLOPE + HJ]
        ident_bf = cbf[:, 0:P]
        future_qk = cbf[:, P:2 * P]
        future_kq = cbf[:, 2 * P:3 * P]
        PS_PV = 7

        def tiles(ap):
            return ap.rearrange("o (c p) d -> p (o c) d", p=P)

        def row_vector(col):
            return vec[:, col:col + D].unsqueeze(1).broadcast_to([P, C, D])

        def token_bank(n):
            return ps[:, n, :].rearrange("p (c d) -> p c d", d=D)

        def decays_of(c):
            return dec[:, c % 2, :, :].rearrange("p (h j) t -> p h j t", j=J)

        def decayed_scores(eng, c, h0):
            return eng.tensor_tensor(am[:, h0:h0 + 4, :, :], decays_of(c)[:, h0:h0 + 4],
                                     gm[:, h0:h0 + 4, :].unsqueeze(2).broadcast_to([P, 4, J, P]), ALU.mult)

        def run(eng, front, back):
            interleave(front(0, True))
            with eng.Fori(0, B - 1) as b:
                interleave(front(b + 1, False), back(b))
            interleave(back(B - 1))

        block = ctx.enter_context(nc.Block())

        @block.sync
        def _(sp):
            sp.dma_start(x0[:, :, :], tiles(x[0:1])).then_inc(x_in, 16)
            sp.dma_start(cst[:, :], consts).then_inc(loaded, 16)
            sp.dma_start(w[:, :], weights).then_inc(loaded, 16)
            sp.dma_start(vec[:, :], vectors.partition_broadcast(P)).then_inc(loaded, 16)
            sp.dma_start(cbf[:, :], consts_bf).then_inc(loaded, 16)
            sp.sem_inc(out_free, 1)

            def next_x(f):
                sp.wait_ge(x1_ready, f + 1)
                sp.dma_start(x0[:, :, :], tiles(x[bass.ds(f + 1, 1)])).then_inc(x_in, 16)

            def spill(f):
                for part, ready in enumerate((part0, part1, part2)):
                    sp.wait_ge(ready, f + 1)
                    sp.dma_start(scratch[part], parts[:, part, :]).then_inc(spilled, 16)

            def stack(b):
                sp.wait_ge(spilled, b * 48 + 48)
                for n, (pq, pk) in enumerate(PRODUCTS):
                    for side, (dst, part) in enumerate(((qs, pq), (ks, pk))):
                        src = scratch[part, :, side * T:(side + 1) * T].rearrange("(h d) t -> d h t", d=DA)
                        sp.dma_start(dst[n * DA:(n + 1) * DA, :, :], src).then_inc(stacked, 16)
                sp.wait_ge(mt_ready, b + 1)
                for part in range(3):
                    sp.dma_start(qs[K_MAX + part:K_MAX + part + 1, :, :],
                                 mT[part * HA:(part + 1) * HA, :]).then_inc(mstacked, 16)

            def store(b):
                sp.wait_ge(x4_ready, b + 1)
                sp.dma_start(tiles(out[bass.ds(b, 1)]), x4[:, :, :]).then_inc(stored, 16)

            def store_done(b):
                sp.wait_ge(stored, b * 16 + 16)
                sp.sem_inc(out_free, 1)

            next_x(0)
            spill(0)
            with sp.Fori(0, B - 2) as b:
                stack(b)
                next_x(b + 1)
                store(b)
                spill(b + 1)
                store_done(b)
            stack(B - 2)
            store(B - 2)
            spill(B - 1)
            store_done(B - 2)
            stack(B - 1)
            store(B - 1)
            sp.wait_ge(stored, B * 16)

        @block.gpsimd
        def _(pool):
            pool.memset(half[:, :], -0.5).then_inc(setup, 1)
            pool.memset(vg[:, :, :, :], 0.0).then_inc(setup, 1)
            pool.memset(va[:, :, :, :], 0.0).then_inc(setup, 1)
            pool.memset(state[:, :, :, :, :], 0.0).then_inc(setup, 1)
            pool.memset(qs[:, :, :], 0.0).then_inc(setup, 1)
            pool.memset(ks[:, :, :], 0.0).then_inc(setup, 1)
            pool.memset(mparts[:, :, :], 0.0).then_inc(setup, 1)
            pool.wait_ge(setup, 7)
            pool.memset(va[:, :, :, DA:DA + 1], 1.0).then_inc(setup, 1)
            pool.wait_ge(setup, 8)
            pool.memset(ks[K_MAX:K_ALL, :, :], 1.0).then_inc(setup, 1)
            pool.wait_ge(setup, 9)
            pool.wait_ge(loaded, 64)

            def front(f, first):
                steps = [0]

                def step(ins):
                    steps[0] += 1
                    ins.then_inc(pool_step, 1)
                    pool.wait_ge(pool_step, f * 8 + steps[0])

                def rsqrt(k):
                    pool.wait_ge(var_ready, f * 4 + k)
                    pool.tensor_tensor(fn.rstd[:, :], fn.ve[:, :], half[:, :], ALU.pow).then_inc(rstd_ready, 1)

                def triangles(c):
                    if c >= 2:
                        pool.wait_ge(e_ps, f * 16 + 4 * (c - 1))
                    pool.tensor_tensor(
                        ae[:, c % 2, :, :], alog[:, c, :].unsqueeze(2).broadcast_to([P, HJ, P]),
                        tri.unsqueeze(1).broadcast_to([P, HJ, P]), ALU.mult).then_inc(ae_ready, 1)

                yield at_front(0)
                rsqrt(1)
                yield at_front(7)
                pool.wait_ge(log_ready, f + 1)
                triangles(0)
                for c in range(-1, C):
                    yield at_chunk(c, 0)
                    if c >= 0:
                        pool.wait_ge(gm_ready, f * 8 + 2 * c + 2)
                        pool.wait_ge(dec_ready, f * 16 + 4 * c + 4)
                        decayed_scores(pool, c, 4).then_inc(am_pool, 1)
                    if c + 2 < C:
                        triangles(c + 2)
                yield at_post(1)
                rsqrt(2)
                yield at_post(2)
                pool.wait_ge(hn_ready, f + 1)
                step(pool.tensor_tensor(hres[:, :, :], fn.xn[:, :, :], row_vector(V_LNG), ALU.mult))
                step(pool.tensor_tensor(hres[:, :, :], hres[:, :, :], row_vector(V_LNB), ALU.add))
                pool.tensor_tensor(x1[:, :, :], hres[:, :, :], x0[:, :, :], ALU.add).then_inc(x1_ready, 1)
                yield at_post(3)
                rsqrt(3)
                yield at_post(5)
                rsqrt(4)
                yield at_post(9)
                pool.wait_ge(qkv_ready, f + 1)
                for c in range(C):
                    xa = qkv[:, c, 0:2 * D].rearrange("p (h e) -> p h e", e=DA)
                    lo, hi = xa[:, :, 0:DA // 2], xa[:, :, DA // 2:]
                    cos = cst[:, C_COS + 4 * c:C_COS + 4 * c + 4].unsqueeze(1).broadcast_to([P, 2 * HA, DA // 2])
                    sin = cst[:, C_SIN + 4 * c:C_SIN + 4 * c + 4].unsqueeze(1).broadcast_to([P, 2 * HA, DA // 2])
                    pool.tensor_tensor(ro[:, 0, c], lo, cos, ALU.mult)
                    pool.tensor_tensor(ro[:, 1, c], hi, sin, ALU.mult)
                    pool.tensor_tensor(ro[:, 2, c], hi, cos, ALU.mult)
                    step(pool.tensor_tensor(ro[:, 3, c], lo, sin, ALU.mult))
                xr = qr[:, :, :].rearrange("p c (h e) -> p (c h) e", e=DA)
                rv = ro.rearrange("p n c h e -> p n (c h) e")
                step(pool.tensor_tensor(xr[:, :, 0:DA // 2], rv[:, 0], rv[:, 1], ALU.subtract))
                step(pool.tensor_tensor(xr[:, :, DA // 2:], rv[:, 2], rv[:, 3], ALU.add))
                pool.sem_inc(rope_ready, 1)
                assert steps[0] == 8

            def back(b):
                yield 0
                pool.wait_ge(x2_ready, b + 1)
                pool.tensor_tensor(x2b[:, :, :], x2[:, :, :], row_vector(V_PROJ), ALU.add).then_inc(x2b_ready, 1)
                yield at_tail(4)
                pool.wait_ge(var_back, b + 1)
                pool.tensor_tensor(bn.rstd[:, :], bn.ve[:, :], half[:, :], ALU.pow).then_inc(rstd_back, 1)

            run(pool, front, back)

        @block.scalar
        def _(act):
            act.wait_ge(loaded, 64)

            def front(f, first):
                def transposed(k):
                    act.wait_ge(xnt_ps, f * 3 + k)
                    act.activation(fn.xnt[:, :], ps[:, 0, :], ACT.Copy).then_inc(xnt_ready, 1)

                def decays(c, n):
                    act.wait_ge(e_ps, f * 16 + 4 * c + n + 1)
                    act.activation(dec[:, c % 2, 4 * n:4 * n + 4, :], ps[:, n % 2, :], ACT.Exp).then_inc(dec_ready, 1)

                yield at_front(2)
                transposed(1)
                yield at_front(4)
                act.wait_ge(kv_ps, f + 1)
                act.activation(ek[:, :, :], ps[:, 2:4, :].rearrange("p a (c n) -> p (a c) n", n=2 * D)[:, :, 0:D],
                               ACT.Exp).then_inc(elu_exp, 1)
                yield at_front(5)
                act.wait_ge(gates_in, f + 1)
                act.activation(gex[:, :, 0:2 * HJ], gin[:, :, :], ACT.Exp).then_inc(gates_abs, 1)
                act.activation(gex[:, :, 2 * HJ:], gates[:, :, 2 * HJ:], ACT.Exp, scale=-1.0).then_inc(gates_exp, 1)
                act.wait_ge(gates_abs, f + 1)
                act.activation(bln[:, :, :], gex[:, :, 0:HJ], ACT.Ln, bias=1.0).then_inc(gates_exp, 1)
                yield at_front(6)
                for n in range(2):
                    act.wait_ge(qk_ps, f * 2 + n + 1)
                    act.activation(eq[:, n, :], ps[:, n, :], ACT.Exp).then_inc(elu_exp, 1)
                for c in range(-1, C):
                    if c + 1 < C:
                        yield at_chunk(c, 0)
                        decays(c + 1, 0)
                        decays(c + 1, 1)
                    yield at_chunk(c, 1)
                    if c >= 0:
                        act.wait_ge(y_ps, f * C + c + 1)
                        act.activation(yT[:, :, :, :], ps[:, 3, :], ACT.Copy).then_inc(y_sb, 1)
                    if c + 1 < C:
                        act.wait_ge(pre_ps, f * C + c + 2)
                        act.activation(pdec[:, :, :], ps[:, 2, 0:J * P], ACT.Exp).then_inc(pdec_ready, 1)
                        decays(c + 1, 2)
                        decays(c + 1, 3)
                yield at_post(0)
                act.wait_ge(ynt_ps, f + 1)
                act.activation(ynt, ps[:, 0, :], ACT.Copy).then_inc(ynt_ready, 1)
                yield at_post(4)
                transposed(2)
                yield at_post(6)
                transposed(3)
                yield at_post(10)
                act.wait_ge(qkt_ps, f + 1)
                act.activation(parts[:, 0, :], ps[:, 0:2, :], ACT.Copy).then_inc(part0, 1)
                yield at_post(11)
                act.wait_ge(res1, f + 1)
                act.activation(parts[:, 1, :], resid, ACT.Copy).then_inc(part1, 1)

            def back(b):
                yield at_minus(2)
                act.wait_ge(mt_ps, b + 1)
                act.activation(mT[:, :], ps[:, 4, :].bitcast(BF16)[:, 0:T], ACT.Copy).then_inc(mt_ready, 1)
                for g in range(4):
                    for k, (kt, c0, m) in enumerate(EXP_GROUPS):
                        n = g * NE + k
                        yield at_exp(n)
                        width = T - kt * P
                        if g >= 1:
                            act.wait_ge(pv_ps, b * 16 + 4 * (g - 1) + kt + 1)
                        act.wait_ge(sc_ps, b * 4 * NE + n + 1)
                        act.activation(pT[:, c0:c0 + m, P_OFF[kt]:P_OFF[kt] + width],
                                       ps[:, 4 + n % 3, 0:m * width].rearrange("p (m n) -> p m n", n=width),
                                       ACT.Exp, scale=SCALE).then_inc(probs_ready, 1)
                        if g >= 1 and k == 2:
                            act.wait_ge(pv_ps, b * 16 + 4 * g)
                            act.activation(oT[:, g - 1, :], ps[:, PS_PV, :], ACT.Copy).then_inc(ot_ready, 1)
                yield at_tail(0)
                act.wait_ge(pv_ps, b * 16 + 16)
                act.activation(oT[:, 3, :], ps[:, PS_PV, :], ACT.Copy).then_inc(ot_ready, 1)
                yield at_tail(2)
                act.wait_ge(ct_ps, b + 1)
                act.activation(cT, ps[:, 4, :], ACT.Copy).then_inc(ct_ready, 1)
                yield at_tail(6)
                act.wait_ge(xnt_ps_back, b + 1)
                act.activation(bn.xnt[:, :], ps[:, 6, :], ACT.Copy).then_inc(xnt_back, 1)

            run(act, front, back)

        @block.tensor
        def _(pe):
            pe.wait_ge(loaded, 64)
            pe.wait_ge(setup, 9)
            pe.wait_ge(sign_ready, 1)

            def turn(dst, src):
                for c in range(C):
                    mm = pe.transpose(ps[:, dst, c * P:(c + 1) * P], src[:, c, :], ident)
                return mm

            def project(src, col, dst, width=D):
                for c in range(C):
                    mm = pe.matmul(ps[:, dst, c * width:(c + 1) * width], src[:, c * P:(c + 1) * P], col,
                                   start=True, stop=True)
                return mm

            def front(f, first):
                def exponents(c, n):
                    if n == 0:
                        pe.wait_ge(ae_ready, f * C + c + 1)
                        if c == 0:
                            pe.wait_ge(qk_ready, f + 1)
                    m = 4 * c + n
                    if m >= 2:
                        pe.wait_ge(dec_ready, f * 16 + m - 1)
                    pe.matmul(ps[:, m % 2, :], after, ae[:, c % 2, 4 * n:4 * n + 4, :],
                              start=True, stop=True).then_inc(e_ps, 1)

                def products(c, g):
                    if g == 0:
                        pe.wait_ge(pdec_ready, f * C + c + 1)
                    else:
                        pe.wait_ge(gm_ready, f * 8 + 2 * c + 1)
                    for i in range(4):
                        mm = pe.matmul(ps[:, 2, i * P:(i + 1) * P], kM[:, 4 * g + i, c * P:(c + 1) * P],
                                       qT[:, c * P:(c + 1) * P], start=True, stop=True)
                    mm.then_inc(g_ps, 1)

                yield at_front(2)
                pe.wait_ge(xn_ready, f * 3 + 1)
                turn(0, fn.xn).then_inc(xnt_ps, 1)
                yield at_front(3)
                pe.wait_ge(xnt_ready, f * 3 + 1)
                project(fn.xnt, w[:, W_GATES:W_GATES + N_GATES], 1, N_GATES).then_inc(gates_ps, 1)
                for c in range(C):
                    mm = pe.matmul(ps[:, 2 + c // 2, (c % 2) * 2 * D:(c % 2 + 1) * 2 * D],
                                   fn.xnt[:, c * P:(c + 1) * P], w[:, W_K:W_K + 2 * D], start=True, stop=True)
                mm.then_inc(kv_ps, 1)
                yield at_front(5)
                pe.matmul(ps[:, 0, :], w[:, W_Q:W_Q + D], fn.xnt[:, :], start=True, stop=True).then_inc(qk_ps, 1)
                pe.wait_ge(gates_in, f + 1)
                pe.matmul(ps[:, 1, :], w[:, W_K:W_K + D], fn.xnt[:, :], start=True, stop=True).then_inc(qk_ps, 1)
                for c in range(-1, C):
                    yield at_chunk(c, 0)
                    if 0 <= c < C - 1:
                        pe.wait_ge(kd_ready, f * 3 + c + 1)
                        for j in range(J):
                            mm = pe.matmul(ps[:, 2, j * 136:(j + 1) * 136], kd[:, j, :], vg[:, c, :, 0:DH + 1],
                                           start=True, stop=True)
                        mm.then_inc(su_ps, 1)
                    if c + 1 < C:
                        exponents(c + 1, 0)
                        exponents(c + 1, 1)
                    yield at_chunk(c, 1)
                    if c >= 0:
                        pe.wait_ge(am_dve, f * C + c + 1)
                        pe.wait_ge(am_pool, f * C + c + 1)
                        if c >= 1:
                            pe.wait_ge(qp_ready, f * C + c + 1)
                            pe.wait_ge(state_ready, f * 3 + c)
                            pe.wait_ge(y_ready, f * C + c)
                            for g in range(2):
                                for j in range(J):
                                    pe.matmul(ps[:, 3, (2 * g + j) * P:(2 * g + j + 1) * P],
                                              state[:, c % 2, j, 4 * g:4 * g + 4, :], qp[:, j, :],
                                              start=(g == 0 and j == 0), stop=False, skip_group_check=True)
                        for g in range(2):
                            for i in range(4):
                                mm = pe.matmul(ps[QUAD * i:QUAD * i + QUAD, 3, 256 * g:256 * g + 256],
                                               vg[:, c, 4 * g + i, :], am[:, 4 * g + i, :, :],
                                               start=(c == 0 and g == 0), stop=True, skip_group_check=True,
                                               tile_position=(0, QUAD * i))
                        mm.then_inc(y_ps, 1)
                    if c + 1 < C:
                        if c < 0:
                            pe.wait_ge(vg_ready, f + 1)
                        else:
                            pe.wait_ge(state_ready, f * 3 + c + 1)
                        for j in range(J):
                            mm = pe.matmul(ps[:, 2, j * P:(j + 1) * P], alogx[:, c + 1, j, :], tri,
                                           start=True, stop=True)
                        mm.then_inc(pre_ps, 1)
                        exponents(c + 1, 2)
                        exponents(c + 1, 3)
                    yield at_chunk(c, 2)
                    if c >= 0:
                        pe.wait_ge(y_sb, f * C + c + 1)
                        for g in range(2):
                            for j in range(J):
                                mm = pe.transpose(ps[:, 3, (2 * g + j) * P:(2 * g + j + 1) * P], yT[:, g, j, :],
                                                  ident)
                        mm.then_inc(yt_ps, 1)
                    if c + 1 < C:
                        products(c + 1, 0)
                        yield at_chunk(c, 3)
                        products(c + 1, 1)
                yield at_post(0)
                pe.wait_ge(y_ready, f * C + C)
                turn(0, ytok).then_inc(ynt_ps, 1)
                yield at_post(1)
                pe.wait_ge(ynt_ready, f + 1)
                project(ynt, w[:, W_OUT:W_OUT + D], 1).then_inc(out_ps, 1)
                yield at_post(4)
                pe.wait_ge(xn_ready, f * 3 + 2)
                turn(0, fn.xn).then_inc(xnt_ps, 1)
                yield at_post(5)
                pe.wait_ge(xnt_ready, f * 3 + 2)
                project(fn.xnt, sgn[:, :], 1).then_inc(ffn_ps, 1)
                yield at_post(6)
                pe.wait_ge(xn_ready, f * 3 + 3)
                turn(0, fn.xn).then_inc(xnt_ps, 1)
                yield at_post(7)
                pe.wait_ge(xnt_ready, f * 3 + 3)
                for c in range(C):
                    mm = pe.matmul(ps[:, c, 0:3 * D], fn.xnt[:, c * P:(c + 1) * P], w[:, W_QKV:W_QKV + 3 * D],
                                   start=True, stop=True)
                mm.then_inc(qkv_ps, 1)
                yield at_post(10)
                pe.wait_ge(rope_ready, f + 1)
                for side in range(2):
                    for c in range(C):
                        mm = pe.transpose(ps[:, side, c * P:(c + 1) * P], qr[:, c, side * D:(side + 1) * D], ident)
                mm.then_inc(qkt_ps, 1)

            def back(b):
                for n, (qt, h0, m) in enumerate(MAX_GROUPS):
                    yield at_max(n)
                    if n == 0:
                        pe.wait_ge(stacked, (b + 1) * (16 * 2 * len(PRODUCTS)))
                    if n >= 2:
                        pe.wait_ge(max_done, b * NG + n - 1)
                    width = (qt + 1) * P
                    per = m // 2
                    for i in range(m):
                        o = ps[:, 4 + 2 * (n % 2) + i // per, (i % per) * width:(i % per + 1) * width]
                        pe.matmul(o, qs[0:K_MAX, h0 + i, qt * P:(qt + 1) * P], ks[0:K_MAX, h0 + i, 0:width],
                                  start=True, stop=False, skip_group_check=True)
                        mm = pe.matmul(o[:, qt * P:(qt + 1) * P], ident_bf, future_qk,
                                       start=False, stop=True, skip_group_check=True)
                    mm.then_inc(max_ps, 1)
                yield at_minus(1)
                pe.wait_ge(mparts_ready, b + 1)
                for c in range(C):
                    mm = pe.transpose(ps[:, 4, :].bitcast(BF16)[:, c * P:(c + 1) * P],
                                      mparts[:, c, :], ident_bf)
                mm.then_inc(mt_ps, 1)

                def scores(n):
                    g, (kt, c0, m) = n // NE, EXP_GROUPS[n % NE]
                    if n >= 3:
                        pe.wait_ge(probs_ready, b * 4 * NE + n - 2)
                    width = T - kt * P
                    for i in range(m):
                        h = 4 * g + c0 + i
                        o = ps[:, 4 + n % 3, i * width:(i + 1) * width]
                        pe.matmul(o, ks[0:K_ALL, h, kt * P:(kt + 1) * P], qs[0:K_ALL, h, kt * P:T],
                                  start=True, stop=False, skip_group_check=True)
                        mm = pe.matmul(o[:, 0:P], ident_bf, future_kq, start=False, stop=True, skip_group_check=True)
                    mm.then_inc(sc_ps, 1)

                def values(g, kt):
                    last = max(k for k, e in enumerate(EXP_GROUPS) if e[0] == kt)
                    pe.wait_ge(probs_ready, b * 4 * NE + g * NE + last + 1)
                    if kt == 0 and g >= 1:
                        pe.wait_ge(ot_ready, b * 4 + g)
                    for i in range(4):
                        q = QUAD * i
                        mm = pe.matmul(ps[q:q + QUAD, PS_PV, kt * P:T], va[:, kt, 4 * g + i, :],
                                       pT[:, i, P_OFF[kt]:P_OFF[kt] + T - kt * P],
                                       start=(kt == 0), stop=(kt == C - 1), skip_group_check=True,
                                       tile_position=(0, q))
                    mm.then_inc(pv_ps, 1)

                yield at_minus(4)
                pe.wait_ge(mstacked, b * 48 + 48)
                pe.wait_ge(va_ready, b + 1)
                scores(0)
                scores(1)
                for n in range(4 * NE):
                    yield at_exp(n)
                    if n + 2 < 4 * NE:
                        scores(n + 2)
                    kt, c0, m = EXP_GROUPS[n % NE]
                    if c0 + m == 4:
                        values(n // NE, kt)
                yield at_tail(1)
                pe.wait_ge(ot_ready, b * 4 + 4)
                for c in range(C):
                    for g in range(4):
                        mm = pe.transpose(ps[:, 4 + c, g * P:(g + 1) * P], oT[:, g, c * P:(c + 1) * P], ident)
                mm.then_inc(ctx_ps, 1)
                yield at_tail(2)
                pe.wait_ge(ctx_ready, b + 1)
                turn(4, ctxt).then_inc(ct_ps, 1)
                yield at_tail(3)
                pe.wait_ge(ct_ready, b + 1)
                project(cT, w[:, W_PROJ:W_PROJ + D], 5).then_inc(proj_ps, 1)
                yield at_tail(6)
                pe.wait_ge(xn_back, b + 1)
                turn(6, bn.xn).then_inc(xnt_ps_back, 1)
                yield at_tail(7)
                pe.wait_ge(xnt_back, b + 1)
                project(bn.xnt, sgn[:, :], 7).then_inc(ffn_back, 1)

            run(pe, front, back)

        @block.vector
        def _(dve):
            dve.wait_ge(loaded, 64)
            dve.tensor_scalar(sgn_neg[:, :], w[:, W_FFN:W_FFN + D], 0.0, None, ALU.is_lt).then_inc(front_step, 1)
            dve.wait_ge(front_step, 1)
            dve.scalar_tensor_tensor(sgn[:, :], w[:, W_FFN:W_FFN + D], 0.0, sgn_neg[:, :],
                                     ALU.is_gt, ALU.subtract).then_inc(sign_ready, 1)
            dve.wait_ge(setup, 9)

            class Steps:

                def __init__(self, step_sem, before):
                    self.sem, self.before, self.n = step_sem, before, 0

                def counted(self, ins):
                    self.n += 1
                    ins.then_inc(self.sem, 1)

                def settle(self):
                    dve.wait_ge(self.sem, self.before + self.n)

                def step(self, ins):
                    self.counted(ins)
                    self.settle()

            def over_features(ap, n):
                return ap.unsqueeze(2).broadcast_to([P, ap.shape[1], n])

            def norm_stats(s, src, nb):
                for c in range(C):
                    s.counted(dve.bn_stats(nb.stats[:, c, :], src[:, c, :]))
                s.settle()
                m0, m1, v0, v1 = nb.stats[:, :, 1], nb.stats[:, :, 4], nb.stats[:, :, 2], nb.stats[:, :, 5]
                s.counted(dve.tensor_tensor(nb.mv[:, 0, :], m0, m1, ALU.add))
                s.counted(dve.tensor_tensor(nb.mv[:, 1, :], m0, m1, ALU.subtract))
                s.step(dve.tensor_tensor(nb.mv[:, 2, :], v0, v1, ALU.add))
                s.counted(dve.tensor_scalar(nb.mean[:, :], nb.mv[:, 0, :], 0.5, None, ALU.mult))
                s.counted(dve.scalar_tensor_tensor(nb.mv[:, 3, :], nb.mv[:, 1, :], 0.25, nb.mv[:, 1, :],
                                                   ALU.mult, ALU.mult))
                s.step(dve.tensor_scalar(nb.mv[:, 4, :], nb.mv[:, 2, :], 1.0 / D, LN_EPS, ALU.mult, ALU.add))
                return dve.tensor_tensor(nb.ve[:, :], nb.mv[:, 3, :], nb.mv[:, 4, :], ALU.add)

            def norm_apply(s, src, nb):
                for c in range(C):
                    ins = dve.tensor_scalar(nb.xn[:, c, :], src[:, c, :], nb.mean[:, c:c + 1], nb.rstd[:, c:c + 1],
                                            ALU.subtract, ALU.mult)
                    if c < C - 1:
                        s.counted(ins)
                return ins

            def front(f, first):
                s = Steps(front_step, f * FRONT_STEPS + 1)
                counted, step, settle = s.counted, s.step, s.settle

                yield at_front(0)
                dve.wait_ge(x_in, f * 16 + 16)
                norm_stats(s, x0, fn).then_inc(var_ready, 1)
                yield at_front(1)
                dve.wait_ge(rstd_ready, f * 4 + 1)
                norm_apply(s, x0, fn).then_inc(xn_ready, 1)
                yield at_front(4)
                dve.wait_ge(gates_ps, f + 1)
                step(dve.tensor_tensor(gates[:, :, :], ps[:, 1, 0:C * N_GATES].rearrange("p (c n) -> p c n", c=C),
                                       vec[:, V_GATES:V_GATES + N_GATES].unsqueeze(1)
                                       .broadcast_to([P, C, N_GATES]), ALU.add))
                beta = gates[:, :, 0:HJ]
                mix = gates[:, :, HJ:2 * HJ].rearrange("p c (h j) -> p c h j", j=J)
                counted(dve.tensor_scalar(bneg[:, :, :], beta, 0.0, None, ALU.min))
                step(dve.tensor_tensor(mmax[:, :, :], mix[:, :, :, 0], mix[:, :, :, 1], ALU.max))
                counted(dve.scalar_tensor_tensor(gin[:, :, 0:HJ], bneg[:, :, :], 2.0, beta, ALU.mult, ALU.subtract))
                dve.tensor_tensor(gin[:, :, HJ:].rearrange("p c (j h) -> p c j h", j=J),
                                  mix.rearrange("p c h j -> p c j h"),
                                  mmax[:, :, :].unsqueeze(2).broadcast_to([P, C, J, H]),
                                  ALU.subtract).then_inc(gates_in, 1)
                yield at_front(5)
                kv = ps[:, 2:4, :].rearrange("p a (c n) -> p (a c) n", n=2 * D)
                dve.wait_ge(elu_exp, f * 3 + 1)
                step(dve.tensor_scalar(ek[:, :, :], ek[:, :, :], 1.0, None, ALU.min))
                counted(dve.scalar_tensor_tensor(ktok[:, :, :], kv[:, :, 0:D], 0.0, ek[:, :, :], ALU.max, ALU.add))
                yield at_front(6)
                dve.wait_ge(gates_exp, f * 2 + 2)
                step(dve.tensor_tensor(bneg[:, :, :], bneg[:, :, :], bln[:, :, :], ALU.subtract))
                step(dve.tensor_tensor(bneg[:, :, :], bneg[:, :, :],
                                       slope.unsqueeze(1).broadcast_to([P, C, HJ]), ALU.subtract))
                step(dve.tensor_scalar(alog[:, :, :], bneg[:, :, :], BETA_CAP, None, ALU.min))
                for c in range(C):
                    ins = dve.tensor_copy(alogx[:, c, :, :].rearrange("p j (h d) -> p j h d", d=DH),
                                          alog[:, c, :].rearrange("p (h j) -> p j h", j=J)
                                          .unsqueeze(3).broadcast_to([P, J, H, DH]))
                    if c < C - 1:
                        counted(ins)
                ins.then_inc(log_ready, 1)
                yield at_front(7)
                counted(dve.tensor_scalar(gsig[:, :, :], gex[:, :, 2 * HJ:], 1.0, None, ALU.add))
                mexp = gex[:, :, HJ:2 * HJ].rearrange("p c (j h) -> p c j h", j=J)
                step(dve.tensor_tensor(mmax[:, :, :], mexp[:, :, 0, :], mexp[:, :, 1, :], ALU.add))
                counted(dve.reciprocal(gsig[:, :, :], gsig[:, :, :]))
                step(dve.reciprocal(mmax[:, :, :], mmax[:, :, :]))
                counted(dve.tensor_tensor(mixw[:, :, :, :], mexp,
                                          mmax[:, :, :].unsqueeze(2).broadcast_to([P, C, J, H]), ALU.mult))
                counted(dve.tensor_copy(vg[:, :, :, DH], gsig[:, :, :]))
                for c in range(C):
                    ins = dve.tensor_tensor(vg[:, c, :, 0:DH], kv[:, c, D:2 * D].rearrange("p (h d) -> p h d", d=DH),
                                            over_features(gsig[:, c, :], DH), ALU.mult)
                    if c < C - 1:
                        counted(ins)
                ins.then_inc(vg_ready, 1)
                yield at_front(8)
                for n, dst in enumerate((qT, kT)):
                    dve.wait_ge(elu_exp, f * 3 + 2 + n)
                    step(dve.tensor_scalar(eq[:, n, :], eq[:, n, :], 1.0, None, ALU.min))
                    step(dve.scalar_tensor_tensor(dst[:, :], ps[:, n, :], 0.0, eq[:, n, :], ALU.max, ALU.add))
                for h in range(H):
                    ins = dve.tensor_scalar(kM[:, h, :], kT[:, :], headmask[:, h:h + 1], None, ALU.mult)
                    if h < H - 1:
                        counted(ins)
                ins.then_inc(qk_ready, 1)

                def masked(c, g):
                    dve.wait_ge(g_ps, f * 8 + 2 * c + g + 1)
                    dve.tensor_tensor(gm[:, 4 * g:4 * g + 4, :], ps[:, 2, :].rearrange("p (h t) -> p h t", t=P),
                                      tri.unsqueeze(1).broadcast_to([P, 4, P]), ALU.mult).then_inc(gm_ready, 1)

                for c in range(-1, C):
                    if c >= 0:
                        yield at_chunk(c, 0)
                        dve.wait_ge(gm_ready, f * 8 + 2 * c + 2)
                        decayed_scores(dve, c, 0).then_inc(am_dve, 1)
                    if 0 <= c < C - 1:
                        yield at_chunk(c, 1)
                        dve.wait_ge(su_ps, f * 3 + c + 1)
                        old, dst = (state[:, n % 2, :, :, 0:DH + 1] for n in (c, c + 1))
                        su = ps[:, 2, 0:J * 136].rearrange("p (j h e) -> p (j h) e", j=J, e=DH + 1)
                        hm = headmask.unsqueeze(2).broadcast_to([P, H, DH + 1])
                        for j in range(J):
                            o = dst[:, j] if c == 0 else sadd[:, j]
                            ins = dve.tensor_tensor(o, su[:, j * H:(j + 1) * H, :], hm, ALU.mult)
                            if c > 0 or j == 0:
                                counted(ins)
                        if c > 0:
                            settle()
                            for j in range(J):
                                ins = dve.scalar_tensor_tensor(dst[:, j], old[:, j], pdec[:, j, P - 1:P],
                                                               sadd[:, j], ALU.mult, ALU.add)
                                if j == 0:
                                    counted(ins)
                        ins.then_inc(state_ready, 1)
                    yield at_chunk(c, 2)
                    if c >= 0:
                        dve.wait_ge(yt_ps, f * C + c + 1)
                        yv = ps[:, 3, :].rearrange("p (n e) -> p n e", e=QUAD)
                        step(dve.tensor_scalar(rec[:, :], yv[:, :, DH], DEN_EPS, None, ALU.add))
                        step(dve.reciprocal(rec[:, :], rec[:, :]))
                        r4 = rec[:, :].rearrange("p (g j i) -> p g j i", g=2, j=J)
                        step(dve.tensor_tensor(r4, r4, mixw[:, c, :, :].rearrange("p j (g i) -> p g j i", g=2),
                                               ALU.mult))
                        step(dve.tensor_tensor(ytmp[:, :, :], yv[:, :, 0:DH], over_features(rec[:, :], DH),
                                               ALU.mult))
                        yj = ytmp[:, :, :].rearrange("p (g j i) e -> p g j (i e)", g=2, j=J)
                        dve.tensor_tensor(ytok[:, c, :].rearrange("p (g n) -> p g n", g=2), yj[:, :, 0, :],
                                          yj[:, :, 1, :], ALU.add).then_inc(y_ready, 1)
                    if c + 1 < C:
                        masked(c + 1, 0)
                        yield at_chunk(c, 3)
                        masked(c + 1, 1)
                        dve.wait_ge(dec_ready, f * 16 + 4 * (c + 1) + 4)
                        if c + 1 < C - 1:
                            for j in range(J):
                                ins = dve.tensor_tensor(kd[:, j, :].rearrange("p (h d) -> p h d", d=DH),
                                                        ktok[:, c + 1, :].rearrange("p (h d) -> p h d", d=DH),
                                                        over_features(decays_of(c + 1)[:, :, j, P - 1], DH),
                                                        ALU.mult)
                                if j == 0:
                                    counted(ins)
                            ins.then_inc(kd_ready, 1)
                        dve.wait_ge(pdec_ready, f * C + c + 2)
                        dve.tensor_tensor(qp[:, :, :], pdec[:, :, :],
                                          qT[:, (c + 1) * P:(c + 2) * P].unsqueeze(1).broadcast_to([P, J, P]),
                                          ALU.mult).then_inc(qp_ready, 1)

                yield at_post(1)
                dve.wait_ge(out_ps, f + 1)
                step(dve.tensor_tensor(hres[:, :, :], token_bank(1), fn.xn[:, :, :], ALU.add))
                step(dve.tensor_tensor(hres[:, :, :], hres[:, :, :], row_vector(V_BOUT), ALU.add))
                norm_stats(s, hres, fn).then_inc(var_ready, 1)
                yield at_post(2)
                dve.wait_ge(rstd_ready, f * 4 + 2)
                norm_apply(s, hres, fn).then_inc(hn_ready, 1)
                yield at_post(3)
                dve.wait_ge(x1_ready, f + 1)
                norm_stats(s, x1, fn).then_inc(var_ready, 1)
                yield at_post(4)
                dve.wait_ge(rstd_ready, f * 4 + 3)
                norm_apply(s, x1, fn).then_inc(xn_ready, 1)
                yield at_post(5)
                dve.wait_ge(ffn_ps, f + 1)
                if not first:
                    dve.wait_ge(x2b_ready, f)
                dve.tensor_tensor(x2[:, :, :], token_bank(1), x1[:, :, :], ALU.add).then_inc(x2_ready, 1)
                dve.wait_ge(x2_ready, f + 1)
                norm_stats(s, x2, fn).then_inc(var_ready, 1)
                yield at_post(6)
                dve.wait_ge(rstd_ready, f * 4 + 4)
                norm_apply(s, x2, fn).then_inc(xn_ready, 1)
                yield at_post(8)
                dve.wait_ge(qkv_ps, f + 1)
                dve.tensor_tensor(qkv, ps[:, 0:4, 0:3 * D],
                                  vec[:, V_QKV:V_QKV + 3 * D].unsqueeze(1).broadcast_to([P, C, 3 * D]),
                                  ALU.add).then_inc(qkv_ready, 1)
                yield at_post(11)
                dve.wait_ge(part0, f + 1)
                dve.tensor_tensor(resid.rearrange("p (a t) -> p a t", a=2), ps[:, 0:2, :],
                                  parts[:, 0, :].rearrange("p (a t) -> p a t", a=2), ALU.subtract).then_inc(res1, 1)
                yield at_post(12)
                dve.wait_ge(part1, f + 1)
                dve.tensor_tensor(parts[:, 2, :], resid, parts[:, 1, :], ALU.subtract).then_inc(part2, 1)
                if not first:
                    dve.wait_ge(pv_ps, f * 16)
                dve.tensor_copy(va[:, :, :, 0:DA],
                                qkv[:, :, 2 * D:].rearrange("p c (h e) -> p c h e", e=DA)).then_inc(va_ready, 1)
                assert s.n == FRONT_STEPS, s.n

            def back(b):
                s = Steps(back_step, b * BACK_STEPS)
                for n, (qt, h0, m) in enumerate(MAX_GROUPS):
                    yield at_max(n)
                    dve.wait_ge(max_ps, b * NG + n + 1)
                    width = (qt + 1) * P
                    bk = 4 + 2 * (n % 2)
                    if qt >= 2:
                        src = ps[:, bk:bk + 2, 0:width]
                    else:
                        src = ps[:, bk:bk + 2, :].rearrange("p a (m k) -> p (a m) k", k=width)
                    dve.tensor_reduce(mrow[:, qt, h0:h0 + m], src, AX.X, ALU.max).then_inc(max_done, 1)
                yield at_minus(0)
                dve.wait_ge(max_done, b * NG + NG)
                s.step(dve.tensor_scalar(mp[:, :, 0, :], mrow[:, :, :], -1.0, None, ALU.mult))
                s.step(dve.scalar_tensor_tensor(mres[:, :, :], mrow[:, :, :], -1.0, mp[:, :, 0, :],
                                                ALU.mult, ALU.subtract))
                s.step(dve.tensor_copy(mp[:, :, 1, :], mres[:, :, :]))
                dve.tensor_tensor(mp[:, :, 2, :], mres[:, :, :], mp[:, :, 1, :],
                                  ALU.subtract).then_inc(mparts_ready, 1)
                yield at_tail(1)
                dve.wait_ge(ctx_ps, b + 1)
                cv = ps[:, 4:8, :].rearrange("p c (h e) -> p (c h) e", e=QUAD)
                s.step(dve.reciprocal(crec[:, :], cv[:, :, DA]))
                dve.tensor_tensor(ctxt.rearrange("p c (h e) -> p (c h) e", e=DA), cv[:, :, 0:DA],
                                  over_features(crec[:, :], DA), ALU.mult).then_inc(ctx_ready, 1)
                yield at_tail(4)
                dve.wait_ge(proj_ps, b + 1)
                dve.wait_ge(x2b_ready, b + 1)
                s.step(dve.tensor_tensor(x3[:, :, :], token_bank(5), x2b[:, :, :], ALU.add))
                norm_stats(s, x3, bn).then_inc(var_back, 1)
                yield at_tail(5)
                dve.wait_ge(rstd_back, b + 1)
                norm_apply(s, x3, bn).then_inc(xn_back, 1)
                yield at_tail(8)
                dve.wait_ge(ffn_back, b + 1)
                dve.wait_ge(out_free, b + 1)
                dve.tensor_tensor(x4[:, :, :], token_bank(7), x3[:, :, :], ALU.add).then_inc(x4_ready, 1)
                assert s.n == BACK_STEPS, s.n

            run(dve, front, back)


def _alibi_slopes():
    start = 2.0 ** (-2.0 ** (-(math.log2(H) - 3)))
    return np.array([start * start ** i for i in range(H)], np.float32)


def _constants():
    i = np.arange(P)
    c = np.zeros((P, N_C), np.float32)
    c[:, C_ID:C_ID + P] = np.eye(P)
    c[:, C_TRI:C_TRI + P] = i[:, None] <= i[None, :]
    c[:, C_AFTER:C_AFTER + P] = i[:, None] > i[None, :]
    c[:, C_HEAD:C_HEAD + H] = (i // DH)[:, None] == np.arange(H)[None, :]
    c[:, C_SLOPE:C_SLOPE + HJ] = np.repeat(_alibi_slopes(), J)[None, :]
    inv = (1.0 / np.float32(10000.0) ** (np.arange(0, DA, 2, dtype=np.float32) / np.float32(DA))).astype(np.float32)
    ang = (np.arange(T, dtype=np.float32)[:, None] * inv[None, :]).astype(np.float32)
    for t in range(C):
        c[:, C_COS + 4 * t:C_COS + 4 * t + 4] = np.cos(ang[t * P:(t + 1) * P])
        c[:, C_SIN + 4 * t:C_SIN + 4 * t + 4] = np.sin(ang[t * P:(t + 1) * P])
    f = np.zeros((P, 3 * P), np.float32)
    f[:, 0:P] = np.eye(P)
    f[:, P:2 * P] = np.where(i[None, :] > i[:, None], NEG, 0.0)
    f[:, 2 * P:] = np.where(i[:, None] > i[None, :], NEG, 0.0)
    return c, f


def kernel(**inputs):
    import concourse.bacc as _bacc
    from concourse.bass_utils import run_bass_kernel_spmd as _run

    g = {k: np.asarray(v) for k, v in inputs.items()}
    a, c = "L0_attn_a_", "L0_attn_b_"
    weights = np.ascontiguousarray(np.concatenate(
        [g[a + "Wq"].T, g[a + "Wk"].T, g[a + "Wv"].T, g[a + "Wbeta"].T, g[a + "Wmix"].T, g[a + "Wgate"].T,
         g[a + "Wout"].T, g["L0_ffn_weight"].T, g[c + "qkv_w"].T, g[c + "proj_w"].T], axis=1))
    vectors = np.concatenate([g[a + "bbeta"], g[a + "bmix"], g[a + "bgate"], g[a + "bout"], g[a + "ln_g"],
                              g[a + "ln_b"], g[c + "qkv_b"], g[c + "proj_b"]])
    cf, cb = _constants()
    arrays = {"x": np.ascontiguousarray(g[a + "x"]), "weights": weights, "vectors": vectors, "consts": cf,
              "consts_bf": cb.astype(mybir.dt.np(BF16))}
    nc = _bacc.Bacc("TRN2", target_bir_lowering=False, num_devices=1)
    args = {n: nc.dram_tensor(n, v.shape, mybir.dt.from_np(v.dtype), kind="ExternalInput").ap()
            for n, v in arrays.items()}
    scratch = nc.dram_tensor("scratch", (3, P, 2 * T), BF16).ap()
    out = nc.dram_tensor("out", (B, T, D), F32, kind="ExternalOutput").ap()
    hybrid_block(nc, args["x"], args["weights"], args["vectors"], args["consts"], args["consts_bf"], scratch, out)
    r = _run(nc, [arrays], core_ids=[0])
    return r.results[0]["out"]
```

```python
import math
from contextlib import ExitStack

import numpy as np

import concourse.bass as bass
from concourse import mybir

F32 = mybir.dt.float32
BF16 = mybir.dt.bfloat16
ALU = mybir.AluOpType
ACT = mybir.ActivationFunctionType
AX = mybir.AxisListType

B, T, D = 8, 512, 128
P = 128
C = T // P
H, J, DH = 8, 2, 16
HJ = H * J
QUAD = 32
HA, DA = 16, 8
LN_EPS = 1e-5
DEN_EPS = 1e-6
BETA_CAP = math.log(0.9999)
SCALE = 1.0 / math.sqrt(DA)
NEG = -3.0e38

W_Q, W_K, W_V = 0, 128, 256
W_GATES = 384
N_GATES = 2 * HJ + H
W_OUT = W_GATES + N_GATES
W_FFN = W_OUT + D
W_QKV = W_FFN + D
W_PROJ = W_QKV + 3 * D
N_W = W_PROJ + D
N_TOK = 2 * D + N_GATES

V_GATES, V_BOUT, V_LNG, V_LNB, V_QKV = 0, 40, 168, 296, 424
V_PROJ = V_QKV + 3 * D
N_V = V_PROJ + D

C_ID, C_TRI, C_AFTER = 0, 128, 256
C_HEAD = 384
C_SLOPE = C_HEAD + H
C_COS = C_SLOPE + HJ
C_SIN = C_COS + C * DA // 2
N_C = C_SIN + C * DA // 2

PARTS = 3
K_COPIES = [(PARTS * DA * r, 0, PARTS) for r in range(PARTS)]
Q_COPIES = [c for r in range(PARTS) for c in ((PARTS * DA * r, r, PARTS - r),
                                              (PARTS * DA * r + (PARTS - r) * DA, 0, r)) if c[2]]
K_MAX = 96
K_ALL = K_MAX + 3

MAX_GROUPS = [(qt, h, n) for qt, n in enumerate((4, 2, 1, 1)) for h in range(0, HA, n)]
NG = len(MAX_GROUPS)
EXP_GROUPS = [(kt, c0, n) for kt, n in enumerate((1, 1, 2, 4)) for c0 in range(0, 4, n)]
NE = len(EXP_GROUPS)
P_OFF = [0, 512, 896, 1152]
P_LEN = 1280

SCAN_STEPS = 63
MID_STEPS = 45
MAX_STEPS = 3
ATTN_STEPS = 18

PE_FILL = (
    "mmsssssmmssssmsmsmsmmsssssssmsmsssssssxsxxxsxxxsssxxsxxxxxsxxxxxssxxxssxxxssxsxxssxxxsxxxxxxxxxxxssx"
    "xsx"
)
PE_ORDER = (
    "mmaasaassasaaasaaaaamaaaamaassaaaasaasaaamsaaaamasaamaaamasaaaasaaaasamassasasasasamaaaamaaasaasaasa"
    "ssssssxxaxxxaxssxxxsxxxsxxxsxsxsxxxsxxxssxsxxxsxxsxsxxxxxxxxsxxxxsxsxsx"
)
PE_DRAIN = (
    "mmaaaaaaaaaaaaaaaaaaamamaaaaaaaaaaamaamaamamaaamaaaaaaaaaamaaaamaaaaaaaaaaaaaxxxxxxxxxxxxaxxxxxxxaxx"
    "xxxxxxxxxxxxxxxxxxxxxxxx"
)
ACT_FILL = "msssssmssssmsssssssmsmmmsssssssssssssssssx"
ACT_ORDER = "maasasassaaaasaaamsaaaaasasaaaasasamaaaaaasaaasaaaaaaaassssaaasamaaammamssassssssasssssssssx"
ACT_DRAIN = "maaaaaaaaaaaaaamaaaaaaaaaamaaaaaaaaaaaaaaaamaaamaamaamaaax"
DVE_FILL = "ssmsmmssmssmmmmsmsmssmssmmmsmmmssssmssxxxxxxxssxxsxxxsxxsxxxxxsxxxsxxxxxssxxxxxxsxxxxxxsxsxxxxxs"
DVE_ORDER = (
    "ssmsmsmsmssmmmmsmmsssssmmmmsmmamasasassssaaxxxxxmxasxxxsxxsxsxsxsxxxxxxsxxxxxxxxxsxxxxxxsxxxsxsxsxxx"
    "xxs"
)
DVE_DRAIN = "mmmmmmmmmmmmmmmmmaaaaaxxxaxxxxxxxxxxxmxxxxxaxxxxxxxxxxxxxxxxxxxxxxxxxx"
POOL_FILL = "smmssmsssmxssssssss"
POOL_ORDER = "smmsssmssmssssasxsss"
POOL_DRAIN = "mmmmax"

def interleave(order, **rows):
    for row in rows.values():
        next(row)
    for letter in order:
        if letter in rows:
            next(rows[letter], None)


def hybrid_block(nc, x, weights, vectors, consts, consts_bf, ones, scratch, out):
    with ExitStack() as ctx:
        def sb(name, shape, dt=F32):
            return ctx.enter_context(nc.sbuf_tensor(name, shape, dt))

        def sem(name):
            return ctx.enter_context(nc.semaphore(name))

        ps = ctx.enter_context(nc.psum_tensor("ps", [P, 8, 512], F32))

        w = sb("w", [P, N_W])
        vec = sb("vec", [P, N_V])
        cst = sb("cst", [P, N_C])
        cbf = sb("cbf", [P, 3 * P], BF16)
        sgn = sb("sgn", [P, D])
        sgn_neg = sb("sgn_neg", [P, D])
        half = sb("half", [P, C])
        x0 = sb("x0", [P, C, D])
        xb = sb("xb", [P, C, D])
        xnb = sb("xnb", [P, C, D])
        x1 = sb("x1", [P, C, D])
        x2 = sb("x2", [P, C, D])
        xk = sb("xk", [P, C, D])

        class Norm:

            def __init__(self, side):
                self.xn = sb(side + "_xn", [P, C, D])
                self.xnt = sb(side + "_xnt", [P, T])
                self.stats = sb(side + "_stats", [P, C, 6])
                self.mv = sb(side + "_mv", [P, 5, C])
                self.mean = sb(side + "_mean", [P, C])
                self.ve = sb(side + "_ve", [P, C])
                self.rstd = sb(side + "_rstd", [P, C])

        sn, mn, an = Norm("scan"), Norm("mid"), Norm("attn")
        qT = sb("qT", [P, T])
        kT = sb("kT", [P, T])
        kM = sb("kM", [P, H, P])
        ktok = sb("ktok", [P, C, D])
        gates = sb("gates", [P, C, N_GATES])
        gin = sb("gin", [P, C, 2 * HJ])
        bneg = sb("bneg", [P, C, HJ])
        mmax = sb("mmax", [P, C, H])
        gex = sb("gex", [P, C, 2 * HJ + H])
        bln = sb("bln", [P, C, HJ])
        alog = sb("alog", [P, C, HJ])
        alogx = sb("alogx", [P, C, J, D])
        gsig = sb("gsig", [P, C, H])
        mixw = sb("mixw", [P, C, J, H])
        vg = sb("vg", [P, C, H, QUAD])
        ae = sb("ae", [P, HJ, P])
        dec = sb("dec", [P, 2, HJ, P])
        gm = sb("gm", [P, H, P])
        am_flat = sb("am_flat", [P, HJ * P])
        am = am_flat[:, :].rearrange("p (h j t) -> p h j t", j=J, t=P)
        eq = am_flat[:, 0:2 * T].rearrange("p (n t) -> p n t", n=2)
        ek = am_flat[:, 2 * T:3 * T].rearrange("p (c d) -> p c d", d=D)
        pdec = sb("pdec", [P, J, P])
        qp = sb("qp", [P, J, P])
        kd = sb("kd", [P, J, D])
        sadd = sb("sadd", [P, J, H, DH + 1])
        state = sb("state", [P, 2, J, H, QUAD])
        yT = sb("yT", [P, 2, J, P])
        rec = sb("rec", [P, HJ])
        ytmp = sb("ytmp", [P, HJ, DH])
        ytok = sb("ytok", [P, C, D])
        hres = sb("hres", [P, C, D])
        ynt = hres[:, :, :].rearrange("p c d -> p (c d)")
        qkv = sb("qkv", [P, C, 3 * D])
        ro = sb("ro", [P, 2, C, 2 * HA, DA // 2])
        qr = sb("qr", [P, C, 2 * D])
        resid = ro[:, :, :, :, :].rearrange("p s c h e -> p s (c h e)")
        parts = sb("parts", [P, 3, 2 * T], BF16)
        qs = sb("qs", [P, HA, T], BF16)
        ks = sb("ks", [P, HA, T], BF16)
        va = sb("va", [P, C, HA, QUAD])
        mrow = sb("mrow", [P, C, HA])
        mres = sb("mres", [P, C, HA])
        mparts = sb("mparts", [P, C, P], BF16)
        mp = mparts[:, :, 0:3 * HA].rearrange("p c (n h) -> p c n h", n=3)
        mT = sb("mT", [P, T], BF16)
        pT = sb("pT", [P, 4, P_LEN])
        oT = sb("oT", [P, 4, T])
        crec = sb("crec", [P, C, HA])
        cT = pT[:, 0, 0:T]
        ctxt = pT[:, 1, 0:T].rearrange("p (c d) -> p c d", d=D)

        loaded = sem("loaded")
        x_in = sem("x_in")
        ones_in = sem("ones_in")
        setup = sem("setup")
        zeroed = sem("zeroed")
        sign_ready = sem("sign_ready")
        scan_step = sem("scan_step")
        var_scan = sem("var_scan")
        rstd_scan = sem("rstd_scan")
        xn_scan = sem("xn_scan")
        xnt_ps = sem("xnt_ps")
        xnt_scan = sem("xnt_scan")
        gates_ps = sem("gates_ps")
        kv_ps = sem("kv_ps")
        qk_ps = sem("qk_ps")
        elu_exp = sem("elu_exp")
        gates_in = sem("gates_in")
        gates_abs = sem("gates_abs")
        gates_exp = sem("gates_exp")
        log_ready = sem("log_ready")
        qk_ready = sem("qk_ready")
        km_ready = sem("km_ready")
        vg_ready = sem("vg_ready")
        ae_ready = sem("ae_ready")
        e_ps = sem("e_ps")
        dec_ready = sem("dec_ready")
        pre_ps = sem("pre_ps")
        pdec_ready = sem("pdec_ready")
        g_ps = sem("g_ps")
        gm_ready = sem("gm_ready")
        kd_ready = sem("kd_ready")
        qp_ready = sem("qp_ready")
        am_dve = sem("am_dve")
        am_pool = sem("am_pool")
        su_ps = sem("su_ps")
        state_ready = sem("state_ready")
        y_ps = sem("y_ps")
        y_sb = sem("y_sb")
        yt_ps = sem("yt_ps")
        y_ready = sem("y_ready")
        xb_ready = sem("xb_ready")
        mid_step = sem("mid_step")
        var_mid = sem("var_mid")
        rstd_mid = sem("rstd_mid")
        xn_mid = sem("xn_mid")
        turned = sem("turned")
        turned_sb = sem("turned_sb")
        out_ps = sem("out_ps")
        x1_ready = sem("x1_ready")
        ffn_ps = sem("ffn_ps")
        x2_ready = sem("x2_ready")
        qkv_ps = sem("qkv_ps")
        qkv_ready = sem("qkv_ready")
        rope_pool = sem("rope_pool")
        rope_ready = sem("rope_ready")
        qkt_ps = sem("qkt_ps")
        part0 = sem("part0")
        res1 = sem("res1")
        part1 = sem("part1")
        part2 = sem("part2")
        va_ready = sem("va_ready")
        spilled = sem("spilled")
        max_step = sem("max_step")
        stacked = sem("stacked")
        max_ps = sem("max_ps")
        max_done = sem("max_done")
        mparts_ready = sem("mparts_ready")
        mt_ps = sem("mt_ps")
        mt_ready = sem("mt_ready")
        mstacked = sem("mstacked")
        xk_ready = sem("xk_ready")
        attn_step = sem("attn_step")
        sc_ps = sem("sc_ps")
        probs_ready = sem("probs_ready")
        pv_ps = sem("pv_ps")
        ot_ready = sem("ot_ready")
        ctx_ps = sem("ctx_ps")
        ctx_ready = sem("ctx_ready")
        ct_ps = sem("ct_ps")
        ct_ready = sem("ct_ready")
        proj_ps = sem("proj_ps")
        var_attn = sem("var_attn")
        rstd_attn = sem("rstd_attn")
        xn_attn = sem("xn_attn")
        xnt_ps_attn = sem("xnt_ps_attn")
        xnt_attn = sem("xnt_attn")
        ffn_attn = sem("ffn_attn")
        out_ready = sem("out_ready")
        stored = sem("stored")
        out_free = sem("out_free")

        ident = cst[:, C_ID:C_ID + P]
        tri = cst[:, C_TRI:C_TRI + P]
        after = cst[:, C_AFTER:C_AFTER + P]
        headmask = cst[:, C_HEAD:C_HEAD + H]
        slope = cst[:, C_SLOPE:C_SLOPE + HJ]
        ident_bf = cbf[:, 0:P]
        future_qk = cbf[:, P:2 * P]
        future_kq = cbf[:, 2 * P:3 * P]
        PS_MID, PS_A, PS_PV = 4, 5, 7
        MAXIMA = (PS_A, PS_A + 1, PS_MID)
        SCORES = (PS_A, PS_A + 1)
        SCORES_LAST = (PS_A, PS_A + 1, PS_MID, 3)

        def tiles(ap):
            return ap.rearrange("o (c p) d -> p (o c) d", p=P)

        def row_vector(col):
            return vec[:, col:col + D].unsqueeze(1).broadcast_to([P, C, D])

        def token_bank(n):
            return ps[:, n, :].rearrange("p (c d) -> p c d", d=D)

        def rotation():
            xa = qkv[:, :, 0:2 * D].rearrange("p c (h e) -> p c h e", e=DA)
            cs = [cst[:, n:n + C * DA // 2].rearrange("p (c e) -> p c e", c=C).unsqueeze(2)
                  .broadcast_to([P, C, 2 * HA, DA // 2]) for n in (C_COS, C_SIN)]
            return xa[:, :, :, 0:DA // 2], xa[:, :, :, DA // 2:], cs[0], cs[1]

        def decays_of(c):
            return dec[:, c % 2, :, :].rearrange("p (h j) t -> p h j t", j=J)

        def decayed_scores(eng, c, h0):
            return eng.tensor_tensor(am[:, h0:h0 + 4, :, :], decays_of(c)[:, h0:h0 + 4],
                                     gm[:, h0:h0 + 4, :].unsqueeze(2).broadcast_to([P, 4, J, P]), ALU.mult)

        def run(scan, mid, maxima, attn, eng, fill, order, drain):
            interleave(order, s=scan(0, True))
            interleave(fill, s=scan(1, False), m=mid(0, True), x=maxima(0, True))
            with eng.Fori(0, B - 2) as b:
                interleave(order, s=scan(b + 2, False), m=mid(b + 1, False), x=maxima(b + 1, False), a=attn(b))
            interleave(drain, m=mid(B - 1, False), x=maxima(B - 1, False), a=attn(B - 2))
            interleave(order, a=attn(B - 1, SCORES_LAST))

        block = ctx.enter_context(nc.Block())

        @block.sync
        def _(sp):
            sp.dma_start(x0[:, :, :], tiles(x[0:1])).then_inc(x_in, 16)
            sp.dma_start(cst[:, :], consts).then_inc(loaded, 16)
            sp.dma_start(w[:, :], weights).then_inc(loaded, 16)
            sp.dma_start(vec[:, :], vectors.partition_broadcast(P)).then_inc(loaded, 16)
            sp.dma_start(cbf[:, :], consts_bf).then_inc(loaded, 16)
            sp.dma_start(ks[K_MAX:K_ALL, :, :], ones).then_inc(ones_in, 16)
            sp.sem_inc(out_free, 1)

            def next_x(f):
                sp.wait_ge(xb_ready, f * 2 + 2)
                sp.dma_start(x0[:, :, :], tiles(x[bass.ds(f + 1, 1)])).then_inc(x_in, 16)

            def spill(m):
                for part, ready in enumerate((part0, part1, part2)):
                    sp.wait_ge(ready, m * 2 + 2)
                    sp.dma_start(scratch[:, part], parts[:, part, :]).then_inc(spilled, 16)

            def stack(m, first=False):
                sp.wait_ge(spilled, m * 48 + 48)
                if not first:
                    sp.wait_ge(sc_ps, m * 4 * NE)
                by_part = scratch.rearrange("h p d t -> (p d) h t")
                for side, (dst, copies) in enumerate(((qs, Q_COPIES), (ks, K_COPIES))):
                    for row, part, n in copies:
                        sp.dma_start(dst[row:row + n * DA, :, :],
                                     by_part[part * DA:(part + n) * DA, :, side * T:(side + 1) * T]
                                     ).then_inc(stacked, 16)

            def stack_maxima(b):
                sp.wait_ge(mt_ready, b + 1)
                for part in range(3):
                    sp.dma_start(qs[K_MAX + part:K_MAX + part + 1, :, :],
                                 mT[part * HA:(part + 1) * HA, :]).then_inc(mstacked, 16)

            def store(b):
                sp.wait_ge(out_ready, b + 2)
                sp.dma_start(tiles(out[bass.ds(b, 1)]), xk[:, :, :]).then_inc(stored, 16)
                sp.wait_ge(stored, b * 16 + 16)
                sp.sem_inc(out_free, 1)

            next_x(0)
            spill(0)
            stack(0, True)
            next_x(1)
            stack_maxima(0)
            with sp.Fori(0, B - 3) as b:
                spill(b + 1)
                stack(b + 1)
                next_x(b + 2)
                store(b)
                stack_maxima(b + 1)
            for b in (B - 3, B - 2):
                spill(b + 1)
                stack(b + 1)
                store(b)
                stack_maxima(b + 1)
            store(B - 1)

        @block.gpsimd
        def _(pool):
            pool.memset(half[:, :], -0.5).then_inc(setup, 1)
            pool.memset(vg[:, :, :, :], 0.0).then_inc(setup, 1)
            pool.memset(va[:, :, :, :], 0.0).then_inc(setup, 1)
            pool.memset(state[:, :, :, :, :], 0.0).then_inc(setup, 1)
            pool.memset(mparts[:, :, :], 0.0).then_inc(setup, 1)
            pool.wait_ge(setup, 5)
            pool.memset(va[:, :, :, DA:DA + 1], 1.0).then_inc(setup, 1)
            pool.wait_ge(setup, 6)
            pool.wait_ge(loaded, 64)

            def rsqrt(ready, value, nb, done):
                pool.wait_ge(ready, value)
                pool.tensor_tensor(nb.rstd[:, :], nb.ve[:, :], half[:, :], ALU.pow).then_inc(done, 1)

            def scan(f, first):
                def triangles(c, h):
                    if c >= 1:
                        pool.wait_ge(e_ps, f * 16 + 4 * (c - 1) + 2 * (h + 1))
                    pool.tensor_tensor(
                        ae[:, H * h:H * h + H, :],
                        alog[:, c, H * h:H * h + H].unsqueeze(2).broadcast_to([P, H, P]),
                        tri.unsqueeze(1).broadcast_to([P, H, P]), ALU.mult).then_inc(ae_ready, 1)

                yield
                rsqrt(var_scan, f + 1, sn, rstd_scan)
                yield
                pool.wait_ge(log_ready, f + 1)
                triangles(0, 0)
                yield
                triangles(0, 1)
                for c in range(-1, C):
                    if c >= 0:
                        yield
                        pool.wait_ge(gm_ready, f * 8 + 2 * c + 2)
                        pool.wait_ge(dec_ready, f * 16 + 4 * c + 4)
                        decayed_scores(pool, c, 4).then_inc(am_pool, 1)
                    if c + 2 < C:
                        yield
                        triangles(c + 2, 0)
                        yield
                        triangles(c + 2, 1)
                    if c == 0:
                        yield
                        pool.wait_ge(xn_scan, f + 1)
                        if not first:
                            pool.wait_ge(x1_ready, f)
                        pool.tensor_tensor(xb[:, :, :], x0[:, :, :], row_vector(V_LNB), ALU.add).then_inc(xb_ready, 1)
                        pool.tensor_tensor(xnb[:, :, :], sn.xn[:, :, :], row_vector(V_BOUT), ALU.add).then_inc(xb_ready, 1)

            def mid(m, first):
                yield
                rsqrt(var_mid, m * 3 + 1, mn, rstd_mid)
                yield
                rsqrt(var_mid, m * 3 + 2, mn, rstd_mid)
                yield
                rsqrt(var_mid, m * 3 + 3, mn, rstd_mid)
                yield
                pool.wait_ge(qkv_ready, m * 4 + 4)
                lo, hi, cos, sin = rotation()
                pool.tensor_tensor(ro[:, 0], hi, sin, ALU.mult).then_inc(rope_pool, 1)
                pool.tensor_tensor(ro[:, 1], lo, sin, ALU.mult).then_inc(rope_pool, 1)

            def maxima(m, first):
                yield
                pool.wait_ge(x2_ready, m + 1)
                pool.wait_ge(out_free, m + 1)
                pool.tensor_tensor(xk[:, :, :], x2[:, :, :], row_vector(V_PROJ), ALU.add).then_inc(xk_ready, 1)

            def attn(b, banks=SCORES):
                yield
                rsqrt(var_attn, b + 1, an, rstd_attn)

            run(scan, mid, maxima, attn, pool, POOL_FILL, POOL_ORDER, POOL_DRAIN)

        @block.scalar
        def _(act):
            act.wait_ge(loaded, 64)

            def scan(f, first):
                def decays(c, n):
                    act.wait_ge(e_ps, f * 16 + 4 * c + n + 1)
                    act.activation(dec[:, c % 2, 4 * n:4 * n + 4, :], ps[:, n % 2, :], ACT.Exp).then_inc(dec_ready, 1)

                def by_head(c):
                    act.wait_ge(qk_ready, f + 1)
                    if c >= 1 or not first:
                        act.wait_ge(gm_ready, f * 8 + 2 * c)
                    for h in range(H):
                        ins = act.activation(kM[:, h, :], kT[:, c * P:(c + 1) * P], ACT.Copy,
                                             scale=headmask[:, h:h + 1])
                    ins.then_inc(km_ready, 1)

                yield
                act.wait_ge(xnt_ps, f + 1)
                act.activation(sn.xnt[:, :], ps[:, 0, :], ACT.Copy).then_inc(xnt_scan, 1)
                yield
                act.wait_ge(kv_ps, f + 1)
                act.activation(ek, ps[:, 2:4, :].rearrange("p a (c n) -> p (a c) n", n=2 * D)[:, :, 0:D],
                               ACT.Exp).then_inc(elu_exp, 1)
                yield
                act.wait_ge(gates_in, f + 1)
                act.activation(gex[:, :, 0:2 * HJ], gin[:, :, :], ACT.Exp).then_inc(gates_abs, 1)
                act.activation(gex[:, :, 2 * HJ:], gates[:, :, 2 * HJ:], ACT.Exp, scale=-1.0).then_inc(gates_exp, 1)
                yield
                act.wait_ge(gates_abs, f + 1)
                act.activation(bln[:, :, :], gex[:, :, 0:HJ], ACT.Ln, bias=1.0).then_inc(gates_exp, 1)
                for n in range(2):
                    yield
                    act.wait_ge(qk_ps, f * 2 + n + 1)
                    act.activation(eq[:, n, :], ps[:, n, :], ACT.Exp).then_inc(elu_exp, 1)
                for c in range(-1, C):
                    if c + 1 < C:
                        yield
                        decays(c + 1, 0)
                        yield
                        decays(c + 1, 1)
                        yield
                        by_head(c + 1)
                    if c >= 0:
                        yield
                        act.wait_ge(y_ps, f * C + c + 1)
                        act.activation(yT[:, :, :, :], ps[:, 3, :], ACT.Copy).then_inc(y_sb, 1)
                    if c + 1 < C:
                        yield
                        act.wait_ge(pre_ps, f * C + c + 2)
                        act.activation(pdec[:, :, :], ps[:, 2, 0:J * P], ACT.Exp).then_inc(pdec_ready, 1)
                        yield
                        decays(c + 1, 2)
                        yield
                        decays(c + 1, 3)

            def mid(m, first):
                def turn_out(k, dst):
                    act.wait_ge(turned, m * 3 + k)
                    act.activation(dst, ps[:, PS_MID, :], ACT.Copy).then_inc(turned_sb, 1)

                def first_part(side):
                    act.wait_ge(qkt_ps, m * 2 + side + 1)
                    act.activation(parts[:, 0, side * T:side * T + T], ps[:, PS_MID, :], ACT.Copy).then_inc(part0, 1)

                def second_part(side):
                    act.wait_ge(res1, m * 2 + side + 1)
                    act.activation(parts[:, 1, side * T:side * T + T], resid[:, side, :], ACT.Copy).then_inc(part1, 1)

                yield
                turn_out(1, ynt)
                yield
                turn_out(2, mn.xnt[:, :])
                yield
                turn_out(3, mn.xnt[:, :])
                yield
                first_part(0)
                yield
                first_part(1)
                yield
                second_part(0)
                yield
                second_part(1)

            def maxima(m, first):
                yield
                act.wait_ge(mt_ps, m + 1)
                act.activation(mT[:, :], ps[:, PS_A, :].bitcast(BF16)[:, 0:T], ACT.Copy).then_inc(mt_ready, 1)

            def attn(b, banks=SCORES):
                for g in range(4):
                    for k, (kt, c0, m) in enumerate(EXP_GROUPS):
                        n = g * NE + k
                        yield
                        width = T - kt * P
                        if g >= 1:
                            act.wait_ge(pv_ps, b * 16 + 4 * (g - 1) + kt + 1)
                        act.wait_ge(sc_ps, b * 4 * NE + n + 1)
                        act.activation(pT[:, c0:c0 + m, P_OFF[kt]:P_OFF[kt] + width],
                                       ps[:, banks[n % len(banks)], 0:m * width].rearrange("p (m n) -> p m n", n=width),
                                       ACT.Exp, scale=SCALE).then_inc(probs_ready, 1)
                        if g >= 1 and k == 2:
                            yield
                            act.wait_ge(pv_ps, b * 16 + 4 * g)
                            act.activation(oT[:, g - 1, :], ps[:, PS_PV, :], ACT.Copy).then_inc(ot_ready, 1)
                yield
                act.wait_ge(pv_ps, b * 16 + 16)
                act.activation(oT[:, 3, :], ps[:, PS_PV, :], ACT.Copy).then_inc(ot_ready, 1)
                yield
                act.wait_ge(ct_ps, b + 1)
                act.activation(cT, ps[:, PS_PV, :], ACT.Copy).then_inc(ct_ready, 1)
                yield
                act.wait_ge(xnt_ps_attn, b + 1)
                act.activation(an.xnt[:, :], ps[:, PS_PV, :], ACT.Copy).then_inc(xnt_attn, 1)

            run(scan, mid, maxima, attn, act, ACT_FILL, ACT_ORDER, ACT_DRAIN)

        @block.tensor
        def _(pe):
            pe.wait_ge(loaded, 64)
            pe.wait_ge(ones_in, 16)
            pe.wait_ge(setup, 6)
            pe.wait_ge(sign_ready, 2)

            def turn(dst, src):
                for c in range(C):
                    mm = pe.transpose(ps[:, dst, c * P:(c + 1) * P], src[:, c, :], ident)
                return mm

            def project(src, col, dst, width=D):
                for c in range(C):
                    mm = pe.matmul(ps[:, dst, c * width:(c + 1) * width], src[:, c * P:(c + 1) * P], col,
                                   start=True, stop=True)
                return mm

            def scan(f, first):
                def exponents(c, n):
                    if n % 2 == 0:
                        pe.wait_ge(ae_ready, f * 8 + 2 * c + n // 2 + 1)
                        if c == 0 and n == 0:
                            pe.wait_ge(qk_ready, f + 1)
                    m = 4 * c + n
                    if m >= 2:
                        pe.wait_ge(dec_ready, f * 16 + m - 1)
                    pe.matmul(ps[:, m % 2, :], after, ae[:, 4 * n:4 * n + 4, :],
                              start=True, stop=True).then_inc(e_ps, 1)

                def products(c, g):
                    if g == 0:
                        pe.wait_ge(pdec_ready, f * C + c + 1)
                        pe.wait_ge(km_ready, f * C + c + 1)
                    else:
                        pe.wait_ge(gm_ready, f * 8 + 2 * c + 1)
                    for i in range(4):
                        mm = pe.matmul(ps[:, 2, i * P:(i + 1) * P], kM[:, 4 * g + i, :],
                                       qT[:, c * P:(c + 1) * P], start=True, stop=True)
                    mm.then_inc(g_ps, 1)

                yield
                pe.wait_ge(xn_scan, f + 1)
                turn(0, sn.xn).then_inc(xnt_ps, 1)
                yield
                pe.wait_ge(xnt_scan, f + 1)
                project(sn.xnt, w[:, W_GATES:W_GATES + N_GATES], 1, N_GATES).then_inc(gates_ps, 1)
                yield
                for c in range(C):
                    mm = pe.matmul(ps[:, 2 + c // 2, (c % 2) * 2 * D:(c % 2 + 1) * 2 * D],
                                   sn.xnt[:, c * P:(c + 1) * P], w[:, W_K:W_K + 2 * D], start=True, stop=True)
                mm.then_inc(kv_ps, 1)
                yield
                pe.matmul(ps[:, 0, :], w[:, W_Q:W_Q + D], sn.xnt[:, :], start=True, stop=True).then_inc(qk_ps, 1)
                yield
                pe.wait_ge(gates_in, f + 1)
                pe.matmul(ps[:, 1, :], w[:, W_K:W_K + D], sn.xnt[:, :], start=True, stop=True).then_inc(qk_ps, 1)
                for c in range(-1, C):
                    if 0 <= c < C - 1:
                        yield
                        pe.wait_ge(kd_ready, f * 3 + c + 1)
                        for j in range(J):
                            mm = pe.matmul(ps[:, 2, j * 136:(j + 1) * 136], kd[:, j, :], vg[:, c, :, 0:DH + 1],
                                           start=True, stop=True)
                        mm.then_inc(su_ps, 1)
                    if c + 1 < C:
                        yield
                        exponents(c + 1, 0)
                        yield
                        exponents(c + 1, 1)
                    if c >= 0:
                        if c >= 1:
                            yield
                            pe.wait_ge(qp_ready, f * C + c + 1)
                            pe.wait_ge(state_ready, f * 3 + c)
                            pe.wait_ge(y_ready, f * C + c)
                            for g in range(2):
                                for j in range(J):
                                    pe.matmul(ps[:, 3, (2 * g + j) * P:(2 * g + j + 1) * P],
                                              state[:, c % 2, j, 4 * g:4 * g + 4, :], qp[:, j, :],
                                              start=(g == 0 and j == 0), stop=False, skip_group_check=True)
                        yield
                        pe.wait_ge(am_dve, f * C + c + 1)
                        pe.wait_ge(am_pool, f * C + c + 1)
                        for g in range(2):
                            for i in range(4):
                                mm = pe.matmul(ps[QUAD * i:QUAD * i + QUAD, 3, 256 * g:256 * g + 256],
                                               vg[:, c, 4 * g + i, :], am[:, 4 * g + i, :, :],
                                               start=(c == 0 and g == 0), stop=True, skip_group_check=True,
                                               tile_position=(0, QUAD * i))
                        mm.then_inc(y_ps, 1)
                    if c + 1 < C:
                        yield
                        if c < 0:
                            pe.wait_ge(vg_ready, f + 1)
                        else:
                            pe.wait_ge(state_ready, f * 3 + c + 1)
                        for j in range(J):
                            mm = pe.matmul(ps[:, 2, j * P:(j + 1) * P], alogx[:, c + 1, j, :], tri,
                                           start=True, stop=True)
                        mm.then_inc(pre_ps, 1)
                        yield
                        exponents(c + 1, 2)
                        yield
                        exponents(c + 1, 3)
                    if c >= 0:
                        yield
                        pe.wait_ge(y_sb, f * C + c + 1)
                        for g in range(2):
                            for j in range(J):
                                mm = pe.transpose(ps[:, 3, (2 * g + j) * P:(2 * g + j + 1) * P], yT[:, g, j, :],
                                                  ident)
                        mm.then_inc(yt_ps, 1)
                    if c + 1 < C:
                        yield
                        products(c + 1, 0)
                        yield
                        products(c + 1, 1)

            def mid(m, first):
                yield
                pe.wait_ge(y_ready, m * C + C)
                turn(PS_MID, ytok).then_inc(turned, 1)
                yield
                pe.wait_ge(turned_sb, m * 3 + 1)
                project(ynt, w[:, W_OUT:W_OUT + D], PS_MID).then_inc(out_ps, 1)
                yield
                pe.wait_ge(xn_mid, m * 2 + 1)
                turn(PS_MID, mn.xn).then_inc(turned, 1)
                yield
                pe.wait_ge(turned_sb, m * 3 + 2)
                project(mn.xnt, sgn[:, :], PS_MID).then_inc(ffn_ps, 1)
                yield
                pe.wait_ge(xn_mid, m * 2 + 2)
                turn(PS_MID, mn.xn).then_inc(turned, 1)
                for c in range(C):
                    yield
                    if c == 0:
                        pe.wait_ge(turned_sb, m * 3 + 3)
                    else:
                        pe.wait_ge(qkv_ready, m * 4 + c)
                    pe.matmul(ps[:, PS_MID, 0:3 * D], mn.xnt[:, c * P:(c + 1) * P], w[:, W_QKV:W_QKV + 3 * D],
                              start=True, stop=True).then_inc(qkv_ps, 1)
                for side in range(2):
                    yield
                    if side == 0:
                        pe.wait_ge(rope_ready, m + 1)
                    else:
                        pe.wait_ge(res1, m * 2 + 1)
                    for c in range(C):
                        mm = pe.transpose(ps[:, PS_MID, c * P:(c + 1) * P], qr[:, c, side * D:(side + 1) * D], ident)
                    mm.then_inc(qkt_ps, 1)

            def maxima(b, first):
                for n, (qt, h0, m) in enumerate(MAX_GROUPS):
                    yield
                    if n == 0 and not first:
                        pe.wait_ge(probs_ready, b * 4 * NE)
                    if n == 0:
                        pe.wait_ge(stacked, (b + 1) * (16 * (len(Q_COPIES) + len(K_COPIES))))
                    if n >= len(MAXIMA):
                        pe.wait_ge(max_done, b * NG + n - len(MAXIMA) + 1)
                    width = (qt + 1) * P
                    for i in range(m):
                        o = ps[:, MAXIMA[n % len(MAXIMA)], i * width:(i + 1) * width]
                        pe.matmul(o, qs[0:K_MAX, h0 + i, qt * P:(qt + 1) * P], ks[0:K_MAX, h0 + i, 0:width],
                                  start=True, stop=False, skip_group_check=True)
                        mm = pe.matmul(o[:, qt * P:(qt + 1) * P], ident_bf, future_qk,
                                       start=False, stop=True, skip_group_check=True)
                    mm.then_inc(max_ps, 1)
                yield
                pe.wait_ge(mparts_ready, b + 1)
                for c in range(C):
                    mm = pe.transpose(ps[:, PS_A, :].bitcast(BF16)[:, c * P:(c + 1) * P],
                                      mparts[:, c, :], ident_bf)
                mm.then_inc(mt_ps, 1)

            def attn(b, banks=SCORES):
                def scores(n):
                    g, (kt, c0, m) = n // NE, EXP_GROUPS[n % NE]
                    if n >= len(banks):
                        pe.wait_ge(probs_ready, b * 4 * NE + n - len(banks) + 1)
                    width = T - kt * P
                    for i in range(m):
                        h = 4 * g + c0 + i
                        o = ps[:, banks[n % len(banks)], i * width:(i + 1) * width]
                        pe.matmul(o, ks[0:K_ALL, h, kt * P:(kt + 1) * P], qs[0:K_ALL, h, kt * P:T],
                                  start=True, stop=False, skip_group_check=True)
                        mm = pe.matmul(o[:, 0:P], ident_bf, future_kq, start=False, stop=True, skip_group_check=True)
                    mm.then_inc(sc_ps, 1)

                def values(g, kt):
                    last = max(k for k, e in enumerate(EXP_GROUPS) if e[0] == kt)
                    pe.wait_ge(probs_ready, b * 4 * NE + g * NE + last + 1)
                    if kt == 0 and g == 0:
                        pe.wait_ge(out_ready, b + 1)
                    elif kt == 0:
                        pe.wait_ge(ot_ready, b * 4 + g)
                    for i in range(4):
                        q = QUAD * i
                        mm = pe.matmul(ps[q:q + QUAD, PS_PV, kt * P:T], va[:, kt, 4 * g + i, :],
                                       pT[:, i, P_OFF[kt]:P_OFF[kt] + T - kt * P],
                                       start=(kt == 0), stop=(kt == C - 1), skip_group_check=True,
                                       tile_position=(0, q))
                    mm.then_inc(pv_ps, 1)

                yield
                pe.wait_ge(mstacked, b * 48 + 48)
                pe.wait_ge(va_ready, b + 1)
                ahead = len(banks) - 1
                for n in range(ahead):
                    scores(n)
                for n in range(4 * NE):
                    if n + ahead < 4 * NE:
                        yield
                        scores(n + ahead)
                    kt, c0, m = EXP_GROUPS[n % NE]
                    if c0 + m == 4:
                        yield
                        values(n // NE, kt)
                for c in range(C):
                    yield
                    if c == 0:
                        pe.wait_ge(ot_ready, b * 4 + 4)
                    else:
                        pe.wait_ge(ctx_ready, b * 4 + c)
                    for g in range(4):
                        mm = pe.transpose(ps[:, PS_PV, g * P:(g + 1) * P], oT[:, g, c * P:(c + 1) * P], ident)
                    mm.then_inc(ctx_ps, 1)
                yield
                pe.wait_ge(ctx_ready, b * 4 + 4)
                turn(PS_PV, ctxt).then_inc(ct_ps, 1)
                yield
                pe.wait_ge(ct_ready, b + 1)
                project(cT, w[:, W_PROJ:W_PROJ + D], PS_PV).then_inc(proj_ps, 1)
                yield
                pe.wait_ge(xn_attn, b + 1)
                turn(PS_PV, an.xn).then_inc(xnt_ps_attn, 1)
                yield
                pe.wait_ge(xnt_attn, b + 1)
                project(an.xnt, sgn[:, :], PS_PV).then_inc(ffn_attn, 1)

            run(scan, mid, maxima, attn, pe, PE_FILL, PE_ORDER, PE_DRAIN)

        @block.vector
        def _(dve):
            dve.memset(qs[0:K_MAX, :, :].bitcast(F32), 0.0).then_inc(zeroed, 1)

            class Steps:

                def __init__(self, step_sem, before):
                    self.sem, self.before, self.n = step_sem, before, 0

                def counted(self, ins):
                    self.n += 1
                    ins.then_inc(self.sem, 1)

                def settle(self):
                    dve.wait_ge(self.sem, self.before + self.n)

                def step(self, ins):
                    self.counted(ins)
                    self.settle()

            def over_features(ap, n):
                return ap.unsqueeze(2).broadcast_to([P, ap.shape[1], n])

            def norm_stats(s, src, nb):
                for c in range(C):
                    s.counted(dve.bn_stats(nb.stats[:, c, :], src[:, c, :]))
                s.settle()
                m0, m1, v0, v1 = nb.stats[:, :, 1], nb.stats[:, :, 4], nb.stats[:, :, 2], nb.stats[:, :, 5]
                s.counted(dve.tensor_tensor(nb.mv[:, 0, :], m0, m1, ALU.add))
                s.counted(dve.tensor_tensor(nb.mv[:, 1, :], m0, m1, ALU.subtract))
                s.step(dve.tensor_tensor(nb.mv[:, 2, :], v0, v1, ALU.add))
                s.counted(dve.tensor_scalar(nb.mean[:, :], nb.mv[:, 0, :], 0.5, None, ALU.mult))
                s.counted(dve.scalar_tensor_tensor(nb.mv[:, 3, :], nb.mv[:, 1, :], 0.25, nb.mv[:, 1, :],
                                                   ALU.mult, ALU.mult))
                s.step(dve.tensor_scalar(nb.mv[:, 4, :], nb.mv[:, 2, :], 1.0 / D, LN_EPS, ALU.mult, ALU.add))
                return dve.tensor_tensor(nb.ve[:, :], nb.mv[:, 3, :], nb.mv[:, 4, :], ALU.add)

            def norm_apply(s, src, nb):
                for c in range(C):
                    ins = dve.tensor_scalar(nb.xn[:, c, :], src[:, c, :], nb.mean[:, c:c + 1], nb.rstd[:, c:c + 1],
                                            ALU.subtract, ALU.mult)
                    if c < C - 1:
                        s.counted(ins)
                return ins

            def scan(f, first):
                s = Steps(scan_step, f * SCAN_STEPS)
                counted, step, settle = s.counted, s.step, s.settle

                yield
                dve.wait_ge(x_in, f * 16 + 16)
                norm_stats(s, x0, sn).then_inc(var_scan, 1)
                if first:
                    dve.wait_ge(loaded, 64)
                    dve.tensor_scalar(sgn_neg[:, :], w[:, W_FFN:W_FFN + D], 0.0, None,
                                      ALU.is_lt).then_inc(sign_ready, 1)
                    dve.wait_ge(sign_ready, 1)
                    dve.scalar_tensor_tensor(sgn[:, :], w[:, W_FFN:W_FFN + D], 0.0, sgn_neg[:, :],
                                             ALU.is_gt, ALU.subtract).then_inc(sign_ready, 1)
                    dve.sem_inc(out_ready, 1)
                    dve.wait_ge(setup, 6)
                yield
                dve.wait_ge(rstd_scan, f + 1)
                norm_apply(s, x0, sn).then_inc(xn_scan, 1)
                if first:
                    dve.memset(ks[0:K_MAX, :, :].bitcast(F32), 0.0).then_inc(zeroed, 1)
                    dve.wait_ge(zeroed, 2)
                yield
                dve.wait_ge(gates_ps, f + 1)
                step(dve.tensor_tensor(gates[:, :, :], ps[:, 1, 0:C * N_GATES].rearrange("p (c n) -> p c n", c=C),
                                       vec[:, V_GATES:V_GATES + N_GATES].unsqueeze(1)
                                       .broadcast_to([P, C, N_GATES]), ALU.add))
                beta = gates[:, :, 0:HJ]
                mix = gates[:, :, HJ:2 * HJ].rearrange("p c (h j) -> p c h j", j=J)
                counted(dve.tensor_scalar(bneg[:, :, :], beta, 0.0, None, ALU.min))
                step(dve.tensor_tensor(mmax[:, :, :], mix[:, :, :, 0], mix[:, :, :, 1], ALU.max))
                counted(dve.scalar_tensor_tensor(gin[:, :, 0:HJ], bneg[:, :, :], 2.0, beta, ALU.mult, ALU.subtract))
                dve.tensor_tensor(gin[:, :, HJ:].rearrange("p c (j h) -> p c j h", j=J),
                                  mix.rearrange("p c h j -> p c j h"),
                                  mmax[:, :, :].unsqueeze(2).broadcast_to([P, C, J, H]),
                                  ALU.subtract).then_inc(gates_in, 1)
                counted(dve.tensor_tensor(bneg[:, :, :], bneg[:, :, :],
                                          slope.unsqueeze(1).broadcast_to([P, C, HJ]), ALU.subtract))
                yield
                kv = ps[:, 2:4, :].rearrange("p a (c n) -> p (a c) n", n=2 * D)
                dve.wait_ge(elu_exp, f * 3 + 1)
                step(dve.tensor_scalar(ek, ek, 1.0, None, ALU.min))
                counted(dve.scalar_tensor_tensor(ktok[:, :, :], kv[:, :, 0:D], 0.0, ek, ALU.max, ALU.add))
                yield
                dve.wait_ge(gates_exp, f * 2 + 2)
                step(dve.tensor_tensor(bneg[:, :, :], bneg[:, :, :], bln[:, :, :], ALU.subtract))
                dve.tensor_scalar(alog[:, :, :], bneg[:, :, :], BETA_CAP, None, ALU.min).then_inc(log_ready, 1)
                dve.wait_ge(log_ready, f + 1)
                for c in range(C):
                    ins = dve.tensor_copy(alogx[:, c, :, :].rearrange("p j (h d) -> p j h d", d=DH),
                                          alog[:, c, :].rearrange("p (h j) -> p j h", j=J)
                                          .unsqueeze(3).broadcast_to([P, J, H, DH]))
                    counted(ins)
                yield
                counted(dve.tensor_scalar(gsig[:, :, :], gex[:, :, 2 * HJ:], 1.0, None, ALU.add))
                mexp = gex[:, :, HJ:2 * HJ].rearrange("p c (j h) -> p c j h", j=J)
                step(dve.tensor_tensor(mmax[:, :, :], mexp[:, :, 0, :], mexp[:, :, 1, :], ALU.add))
                counted(dve.reciprocal(gsig[:, :, :], gsig[:, :, :]))
                step(dve.reciprocal(mmax[:, :, :], mmax[:, :, :]))
                counted(dve.tensor_tensor(mixw[:, :, :, :], mexp,
                                          mmax[:, :, :].unsqueeze(2).broadcast_to([P, C, J, H]), ALU.mult))
                counted(dve.tensor_copy(vg[:, :, :, DH], gsig[:, :, :]))
                for c in range(C):
                    ins = dve.tensor_tensor(vg[:, c, :, 0:DH], kv[:, c, D:2 * D].rearrange("p (h d) -> p h d", d=DH),
                                            over_features(gsig[:, c, :], DH), ALU.mult)
                    if c < C - 1:
                        counted(ins)
                ins.then_inc(vg_ready, 1)
                yield
                for n, dst in enumerate((qT, kT)):
                    dve.wait_ge(elu_exp, f * 3 + 2 + n)
                    step(dve.tensor_scalar(eq[:, n, :], eq[:, n, :], 1.0, None, ALU.min))
                    ins = dve.scalar_tensor_tensor(dst[:, :], ps[:, n, :], 0.0, eq[:, n, :], ALU.max, ALU.add)
                    if n == 0:
                        counted(ins)
                ins.then_inc(qk_ready, 1)

                def masked(c, g):
                    dve.wait_ge(g_ps, f * 8 + 2 * c + g + 1)
                    dve.tensor_tensor(gm[:, 4 * g:4 * g + 4, :], ps[:, 2, :].rearrange("p (h t) -> p h t", t=P),
                                      tri.unsqueeze(1).broadcast_to([P, 4, P]), ALU.mult).then_inc(gm_ready, 1)

                for c in range(-1, C):
                    if c >= 0:
                        yield
                        dve.wait_ge(gm_ready, f * 8 + 2 * c + 2)
                        decayed_scores(dve, c, 0).then_inc(am_dve, 1)
                    if 0 <= c < C - 1:
                        yield
                        dve.wait_ge(su_ps, f * 3 + c + 1)
                        old, dst = (state[:, n % 2, :, :, 0:DH + 1] for n in (c, c + 1))
                        su = ps[:, 2, 0:J * 136].rearrange("p (j h e) -> p (j h) e", j=J, e=DH + 1)
                        hm = headmask.unsqueeze(2).broadcast_to([P, H, DH + 1])
                        for j in range(J):
                            o = dst[:, j] if c == 0 else sadd[:, j]
                            ins = dve.tensor_tensor(o, su[:, j * H:(j + 1) * H, :], hm, ALU.mult)
                            if c > 0 or j == 0:
                                counted(ins)
                        if c > 0:
                            settle()
                            for j in range(J):
                                ins = dve.scalar_tensor_tensor(dst[:, j], old[:, j], pdec[:, j, P - 1:P],
                                                               sadd[:, j], ALU.mult, ALU.add)
                                if j == 0:
                                    counted(ins)
                        ins.then_inc(state_ready, 1)
                    if c >= 0:
                        yield
                        dve.wait_ge(yt_ps, f * C + c + 1)
                        yv = ps[:, 3, :].rearrange("p (n e) -> p n e", e=QUAD)
                        step(dve.tensor_scalar(rec[:, :], yv[:, :, DH], DEN_EPS, None, ALU.add))
                        step(dve.reciprocal(rec[:, :], rec[:, :]))
                        r4 = rec[:, :].rearrange("p (g j i) -> p g j i", g=2, j=J)
                        step(dve.tensor_tensor(r4, r4, mixw[:, c, :, :].rearrange("p j (g i) -> p g j i", g=2),
                                               ALU.mult))
                        step(dve.tensor_tensor(ytmp[:, :, :], yv[:, :, 0:DH], over_features(rec[:, :], DH),
                                               ALU.mult))
                        yj = ytmp[:, :, :].rearrange("p (g j i) e -> p g j (i e)", g=2, j=J)
                        if c == 0 and not first:
                            dve.wait_ge(turned, f * 3 - 2)
                        dve.tensor_tensor(ytok[:, c, :].rearrange("p (g n) -> p g n", g=2), yj[:, :, 0, :],
                                          yj[:, :, 1, :], ALU.add).then_inc(y_ready, 1)
                    if c + 1 < C:
                        yield
                        masked(c + 1, 0)
                        yield
                        masked(c + 1, 1)
                        if c + 1 < C - 1:
                            yield
                            dve.wait_ge(dec_ready, f * 16 + 4 * (c + 1) + 4)
                            for j in range(J):
                                ins = dve.tensor_tensor(kd[:, j, :].rearrange("p (h d) -> p h d", d=DH),
                                                        ktok[:, c + 1, :].rearrange("p (h d) -> p h d", d=DH),
                                                        over_features(decays_of(c + 1)[:, :, j, P - 1], DH),
                                                        ALU.mult)
                                if j == 0:
                                    counted(ins)
                            ins.then_inc(kd_ready, 1)
                        yield
                        dve.wait_ge(pdec_ready, f * C + c + 2)
                        dve.tensor_tensor(qp[:, :, :], pdec[:, :, :],
                                          qT[:, (c + 1) * P:(c + 2) * P].unsqueeze(1).broadcast_to([P, J, P]),
                                          ALU.mult).then_inc(qp_ready, 1)

                assert s.n == SCAN_STEPS, s.n

            def mid(m, first):
                s = Steps(mid_step, m * MID_STEPS)
                step = s.step

                yield
                dve.wait_ge(xb_ready, m * 2 + 2)
                dve.wait_ge(out_ps, m + 1)
                step(dve.tensor_tensor(hres[:, :, :], token_bank(PS_MID), xnb[:, :, :], ALU.add))
                norm_stats(s, hres, mn).then_inc(var_mid, 1)
                yield
                dve.wait_ge(rstd_mid, m * 3 + 1)
                step(norm_apply(s, hres, mn))
                step(dve.tensor_tensor(hres[:, :, :], mn.xn[:, :, :], row_vector(V_LNG), ALU.mult))
                dve.tensor_tensor(x1[:, :, :], hres[:, :, :], xb[:, :, :], ALU.add).then_inc(x1_ready, 1)
                yield
                dve.wait_ge(x1_ready, m + 1)
                norm_stats(s, x1, mn).then_inc(var_mid, 1)
                yield
                dve.wait_ge(rstd_mid, m * 3 + 2)
                norm_apply(s, x1, mn).then_inc(xn_mid, 1)
                yield
                dve.wait_ge(ffn_ps, m + 1)
                if not first:
                    dve.wait_ge(xk_ready, m)
                dve.tensor_tensor(x2[:, :, :], token_bank(PS_MID), x1[:, :, :], ALU.add).then_inc(x2_ready, 1)
                yield
                dve.wait_ge(x2_ready, m + 1)
                norm_stats(s, x2, mn).then_inc(var_mid, 1)
                yield
                dve.wait_ge(rstd_mid, m * 3 + 3)
                norm_apply(s, x2, mn).then_inc(xn_mid, 1)
                for c in range(C):
                    yield
                    dve.wait_ge(qkv_ps, m * 4 + c + 1)
                    dve.tensor_tensor(qkv[:, c, :], ps[:, PS_MID, 0:3 * D], vec[:, V_QKV:V_QKV + 3 * D],
                                      ALU.add).then_inc(qkv_ready, 1)
                yield
                dve.wait_ge(qkv_ready, m * 4 + 4)
                lo, hi, cos, sin = rotation()
                xr = qr[:, :, :].rearrange("p c (h e) -> p c h e", e=DA)
                s.counted(dve.tensor_tensor(xr[:, :, :, 0:DA // 2], lo, cos, ALU.mult))
                step(dve.tensor_tensor(xr[:, :, :, DA // 2:], hi, cos, ALU.mult))
                yield
                dve.wait_ge(rope_pool, m * 2 + 2)
                s.counted(dve.tensor_tensor(xr[:, :, :, 0:DA // 2], xr[:, :, :, 0:DA // 2], ro[:, 0], ALU.subtract))
                dve.tensor_tensor(xr[:, :, :, DA // 2:], xr[:, :, :, DA // 2:], ro[:, 1],
                                  ALU.add).then_inc(rope_ready, 1)

                def leave_first(side):
                    dve.wait_ge(part0, m * 2 + side + 1)
                    dve.tensor_tensor(resid[:, side, :], ps[:, PS_MID, :], parts[:, 0, side * T:side * T + T],
                                      ALU.subtract).then_inc(res1, 1)

                def third_part(side):
                    dve.wait_ge(part1, m * 2 + side + 1)
                    dve.tensor_tensor(parts[:, 2, side * T:side * T + T], resid[:, side, :],
                                      parts[:, 1, side * T:side * T + T], ALU.subtract).then_inc(part2, 1)

                yield
                leave_first(0)
                yield
                leave_first(1)
                yield
                third_part(0)
                yield
                third_part(1)
                yield
                if not first:
                    dve.wait_ge(pv_ps, m * 16)
                dve.tensor_copy(va[:, :, :, 0:DA],
                                qkv[:, :, 2 * D:].rearrange("p c (h e) -> p c h e", e=DA)).then_inc(va_ready, 1)
                assert s.n == MID_STEPS, s.n

            def maxima(b, first):
                s = Steps(max_step, b * MAX_STEPS)
                for n, (qt, h0, m) in enumerate(MAX_GROUPS):
                    yield
                    dve.wait_ge(max_ps, b * NG + n + 1)
                    width = (qt + 1) * P
                    dve.tensor_reduce(mrow[:, qt, h0:h0 + m],
                                      ps[:, MAXIMA[n % len(MAXIMA)], 0:m * width].rearrange("p (m k) -> p m k", k=width),
                                      AX.X, ALU.max).then_inc(max_done, 1)
                yield
                dve.wait_ge(max_done, b * NG + NG)
                s.step(dve.tensor_scalar(mp[:, :, 0, :], mrow[:, :, :], -1.0, None, ALU.mult))
                s.step(dve.scalar_tensor_tensor(mres[:, :, :], mrow[:, :, :], -1.0, mp[:, :, 0, :],
                                                ALU.mult, ALU.subtract))
                s.step(dve.tensor_copy(mp[:, :, 1, :], mres[:, :, :]))
                dve.tensor_tensor(mp[:, :, 2, :], mres[:, :, :], mp[:, :, 1, :],
                                  ALU.subtract).then_inc(mparts_ready, 1)
                assert s.n == MAX_STEPS, s.n

            def attn(b, banks=SCORES):
                s = Steps(attn_step, b * ATTN_STEPS)
                for c in range(C):
                    yield
                    dve.wait_ge(ctx_ps, b * 4 + c + 1)
                    cv = ps[:, PS_PV, :].rearrange("p (h e) -> p h e", e=QUAD)
                    s.step(dve.reciprocal(crec[:, c, :], cv[:, :, DA]))
                    dve.tensor_tensor(ctxt[:, c, :].rearrange("p (h e) -> p h e", e=DA), cv[:, :, 0:DA],
                                      over_features(crec[:, c, :], DA), ALU.mult).then_inc(ctx_ready, 1)
                yield
                dve.wait_ge(proj_ps, b + 1)
                dve.wait_ge(xk_ready, b + 1)
                s.step(dve.tensor_tensor(xk[:, :, :], token_bank(PS_PV), xk[:, :, :], ALU.add))
                norm_stats(s, xk, an).then_inc(var_attn, 1)
                yield
                dve.wait_ge(rstd_attn, b + 1)
                norm_apply(s, xk, an).then_inc(xn_attn, 1)
                yield
                dve.wait_ge(ffn_attn, b + 1)
                dve.tensor_tensor(xk[:, :, :], token_bank(PS_PV), xk[:, :, :], ALU.add).then_inc(out_ready, 1)
                assert s.n == ATTN_STEPS, s.n

            run(scan, mid, maxima, attn, dve, DVE_FILL, DVE_ORDER, DVE_DRAIN)


def _alibi_slopes():
    start = 2.0 ** (-2.0 ** (-(math.log2(H) - 3)))
    return np.array([start * start ** i for i in range(H)], np.float32)


def _constants():
    i = np.arange(P)
    c = np.zeros((P, N_C), np.float32)
    c[:, C_ID:C_ID + P] = np.eye(P)
    c[:, C_TRI:C_TRI + P] = i[:, None] <= i[None, :]
    c[:, C_AFTER:C_AFTER + P] = i[:, None] > i[None, :]
    c[:, C_HEAD:C_HEAD + H] = (i // DH)[:, None] == np.arange(H)[None, :]
    c[:, C_SLOPE:C_SLOPE + HJ] = np.repeat(_alibi_slopes(), J)[None, :]
    inv = (1.0 / np.float32(10000.0) ** (np.arange(0, DA, 2, dtype=np.float32) / np.float32(DA))).astype(np.float32)
    ang = (np.arange(T, dtype=np.float32)[:, None] * inv[None, :]).astype(np.float32)
    for t in range(C):
        c[:, C_COS + 4 * t:C_COS + 4 * t + 4] = np.cos(ang[t * P:(t + 1) * P])
        c[:, C_SIN + 4 * t:C_SIN + 4 * t + 4] = np.sin(ang[t * P:(t + 1) * P])
    f = np.zeros((P, 3 * P), np.float32)
    f[:, 0:P] = np.eye(P)
    f[:, P:2 * P] = np.where(i[None, :] > i[:, None], NEG, 0.0)
    f[:, 2 * P:] = np.where(i[:, None] > i[None, :], NEG, 0.0)
    return c, f


def kernel(**inputs):
    import concourse.bacc as _bacc
    from concourse.bass_utils import run_bass_kernel_spmd as _run

    g = {k: np.asarray(v) for k, v in inputs.items()}
    a, c = "L0_attn_a_", "L0_attn_b_"
    weights = np.ascontiguousarray(np.concatenate(
        [g[a + "Wq"].T, g[a + "Wk"].T, g[a + "Wv"].T, g[a + "Wbeta"].T, g[a + "Wmix"].T, g[a + "Wgate"].T,
         g[a + "Wout"].T, g["L0_ffn_weight"].T, g[c + "qkv_w"].T, g[c + "proj_w"].T], axis=1))
    vectors = np.concatenate([g[a + "bbeta"], g[a + "bmix"], g[a + "bgate"], g[a + "bout"], g[a + "ln_g"],
                              g[a + "ln_b"], g[c + "qkv_b"], g[c + "proj_b"]])
    cf, cb = _constants()
    arrays = {"x": np.ascontiguousarray(g[a + "x"]), "weights": weights, "vectors": vectors, "consts": cf,
              "consts_bf": cb.astype(mybir.dt.np(BF16)),
              "ones": np.ones((K_ALL - K_MAX, HA, T), mybir.dt.np(BF16))}
    nc = _bacc.Bacc("TRN2", target_bir_lowering=False, num_devices=1)
    args = {n: nc.dram_tensor(n, v.shape, mybir.dt.from_np(v.dtype), kind="ExternalInput").ap()
            for n, v in arrays.items()}
    scratch = nc.dram_tensor("scratch", (HA, PARTS, DA, 2 * T), BF16).ap()
    out = nc.dram_tensor("out", (B, T, D), F32, kind="ExternalOutput").ap()
    hybrid_block(nc, args["x"], args["weights"], args["vectors"], args["consts"], args["consts_bf"], args["ones"],
                 scratch, out)
    r = _run(nc, [arrays], core_ids=[0])
    return r.results[0]["out"]
```
